# Optimizing a Trainium2 kernel written in Bass

```python
import numpy as np
import jax
import jax.numpy as jnp

def _softmax(x, axis=-1):
    return jax.nn.softmax(x, axis=axis)

def _gelu(x):
    return jax.nn.gelu(x, approximate=True)

def _silu(x):
    return jax.nn.silu(x)

def _sigmoid(x):
    return jax.nn.sigmoid(x)

def _layernorm(x, axis=-1, eps=1e-05):
    m = jnp.mean(x, axis=axis, keepdims=True)
    v = jnp.var(x, axis=axis, keepdims=True)
    return (x - m) / jnp.sqrt(v + eps)

def _scatter_add(tgt, idx, src, axis=0):
    return tgt.at[idx].add(src)

def _segment_sum(src, seg, n):
    return jax.ops.segment_sum(src, seg, n)
kernel_name = 'mk_gnn_ffn_d2_gnn_r8_13be2c'

def setup_inputs(seed: int=0):
    np.random.seed(seed)
    _w = jnp.asarray

    def _rec_inputs():
        import jax
        import jax.numpy as jnp
        _gk = jax.random.key(seed)
        x = -0.0003019 + 1 * jax.random.normal(jax.random.fold_in(_gk, 1), (2500, 1024), jnp.float32)
        src = jax.random.randint(jax.random.fold_in(_gk, 2), (40000,), 0, 2500, jnp.int32)
        dst = jnp.minimum((2500 * jax.random.uniform(jax.random.fold_in(_gk, 3), (40000,)) ** 2.0).astype(jnp.int32), 19999)
        _o = jnp.argsort(dst, stable=True)
        src = src[_o]
        dst = dst[_o]
        edge_weight = jax.random.uniform(jax.random.fold_in(_gk, 12), (40000,), jnp.float32, 0.0, 0.999998)
        return (x, src, dst, edge_weight)
    x, src, dst, edge_weight = _rec_inputs()

    def _L0_gnn_setup():
        import jax, jax.numpy as jnp
        import numpy as np
        N_NODES = 2500
        N_EDGES = 40000
        F_IN = 1024
        F_OUT = 1024
        key = jax.random.key(seed)
        k1, k2, k3, k4, k5 = jax.random.split(key, 5)
        x = jax.random.normal(k1, (N_NODES, F_IN), dtype=jnp.float32)
        std = 1.0 / np.sqrt(F_OUT)
        W = jax.random.uniform(k2, (F_IN, F_OUT), minval=-std, maxval=std, dtype=jnp.float32)
        edge_w = jax.random.uniform(k3, (N_EDGES,), dtype=jnp.float32)
        src = jax.random.randint(k4, (N_EDGES,), 0, N_NODES, dtype=jnp.int32)
        dst = jax.random.randint(k5, (N_EDGES,), 0, N_NODES, dtype=jnp.int32)
        return {'x': x, 'W': W, 'edge_w': edge_w, 'src': src, 'dst': dst}
    _L0_gnn_all = _L0_gnn_setup()
    _L0_gnn_in = {k: v for k, v in _L0_gnn_all.items() if k in ('W',)}
    del _L0_gnn_all

    def _L0_ffn_setup():
        import jax, jax.numpy as jnp
        import numpy as np
        LN_EPS = 1e-05

        def layer_norm(x, g, b):
            mu = jnp.mean(x, axis=-1, keepdims=True)
            var = jnp.mean(jnp.square(x - mu), axis=-1, keepdims=True)
            return (x - mu) * jax.lax.rsqrt(var + LN_EPS) * g + b

        def ternary_quant(w):
            scale = 1.0 / jnp.clip(jnp.mean(jnp.abs(w)), 1e-05)
            wq = jnp.clip(jnp.round(w * scale), -1.0, 1.0) / scale
            return w + jax.lax.stop_gradient(wq - w)
        key = jax.random.key(seed)
        ks = jax.random.split(key, 3)
        dim, hidden = (1024, 512)
        B, S = (8, 1024)
        x = jax.random.normal(ks[0], (B, S, dim), dtype=jnp.float32)
        w1 = jax.random.normal(ks[1], (hidden, dim), dtype=jnp.float32) * 0.02
        w2 = jax.random.normal(ks[2], (dim, hidden), dtype=jnp.float32) * 0.02
        return {'x': x, 'ln1_g': jnp.ones((dim,), jnp.float32), 'ln1_b': jnp.zeros((dim,), jnp.float32), 'w1': w1, 'b1': jnp.zeros((hidden,), jnp.float32), 'ln2_g': jnp.ones((hidden,), jnp.float32), 'ln2_b': jnp.zeros((hidden,), jnp.float32), 'w2': w2, 'b2': jnp.zeros((dim,), jnp.float32)}
    _L0_ffn_all = _L0_ffn_setup()
    _L0_ffn_in = {k: v for k, v in _L0_ffn_all.items() if k in ('ln1_g', 'ln1_b', 'w1', 'b1', 'ln2_g', 'ln2_b', 'w2', 'b2')}
    del _L0_ffn_all

    def _L1_gnn_setup():
        import jax, jax.numpy as jnp
        import numpy as np
        N, IN_FEAT, OUT_FEAT, HEADS, E = (2500, 1024, 256, 4, 40000)
        NEG_SLOPE = 0.2
        key = jax.random.key(seed)
        k1, k2, k3, k4, k5, k6 = jax.random.split(key, 6)
        h = jax.random.normal(k1, (N, IN_FEAT), dtype=jnp.float32)
        src = jax.random.randint(k2, (E,), 0, N, dtype=jnp.int32)
        dst = jax.random.randint(k3, (E,), 0, N, dtype=jnp.int32)
        W = jax.random.normal(k4, (HEADS, IN_FEAT, OUT_FEAT), dtype=jnp.float32) * (1.0 / np.sqrt(IN_FEAT))
        a_l = jax.random.normal(k5, (HEADS, OUT_FEAT), dtype=jnp.float32) * (1.0 / np.sqrt(OUT_FEAT))
        a_r = jax.random.normal(k6, (HEADS, OUT_FEAT), dtype=jnp.float32) * (1.0 / np.sqrt(OUT_FEAT))
        return {'h': h, 'W': W, 'a_l': a_l, 'a_r': a_r, 'src': src, 'dst': dst}
    _L1_gnn_all = _L1_gnn_setup()
    _L1_gnn_in = {k: v for k, v in _L1_gnn_all.items() if k in ('W', 'a_l', 'a_r')}
    del _L1_gnn_all

    def _L1_ffn_setup():
        import jax, jax.numpy as jnp
        import numpy as np
        D = 1024
        H = 256
        E = 8
        TOP_K = 2
        N_SHARED = 1
        B, S = (2, 1024)
        key = jax.random.key(seed)
        ks = jax.random.split(key, 12)
        sc = 0.02
        return {'hidden': jax.random.normal(ks[0], (B, S, D), jnp.float32), 'router_w': jax.random.normal(ks[1], (D, E), jnp.float32) * sc, 'router_b': jnp.zeros((E,), jnp.float32), 'sw1': jax.random.normal(ks[2], (D, H), jnp.float32) * sc, 'sb1': jnp.zeros((H,), jnp.float32), 'sw2': jax.random.normal(ks[3], (H, D), jnp.float32) * sc, 'sb2': jnp.zeros((D,), jnp.float32), 'rw1': jax.random.normal(ks[4], (E, D, H), jnp.float32) * sc, 'rb1': jnp.zeros((E, H), jnp.float32), 'rw2': jax.random.normal(ks[5], (E, H, D), jnp.float32) * sc, 'rb2': jnp.zeros((E, D), jnp.float32)}
    _L1_ffn_all = _L1_ffn_setup()
    _L1_ffn_in = {k: v for k, v in _L1_ffn_all.items() if k in ('router_w', 'router_b', 'sw1', 'sb1', 'sw2', 'sb2', 'rw1', 'rb1', 'rw2', 'rb2')}
    del _L1_ffn_all
    return {'x': x, 'src': src, 'dst': dst, 'edge_weight': edge_weight, 'L0_gnn_W': _L0_gnn_in['W'], 'L0_ffn_ln1_g': _L0_ffn_in['ln1_g'], 'L0_ffn_ln1_b': _L0_ffn_in['ln1_b'], 'L0_ffn_w1': _L0_ffn_in['w1'], 'L0_ffn_b1': _L0_ffn_in['b1'], 'L0_ffn_ln2_g': _L0_ffn_in['ln2_g'], 'L0_ffn_ln2_b': _L0_ffn_in['ln2_b'], 'L0_ffn_w2': _L0_ffn_in['w2'], 'L0_ffn_b2': _L0_ffn_in['b2'], 'L1_gnn_W': _L1_gnn_in['W'], 'L1_gnn_a_l': _L1_gnn_in['a_l'], 'L1_gnn_a_r': _L1_gnn_in['a_r'], 'L1_ffn_router_w': _L1_ffn_in['router_w'], 'L1_ffn_router_b': _L1_ffn_in['router_b'], 'L1_ffn_sw1': _L1_ffn_in['sw1'], 'L1_ffn_sb1': _L1_ffn_in['sb1'], 'L1_ffn_sw2': _L1_ffn_in['sw2'], 'L1_ffn_sb2': _L1_ffn_in['sb2'], 'L1_ffn_rw1': _L1_ffn_in['rw1'], 'L1_ffn_rb1': _L1_ffn_in['rb1'], 'L1_ffn_rw2': _L1_ffn_in['rw2'], 'L1_ffn_rb2': _L1_ffn_in['rb2']}

def reference(x, src, dst, edge_weight, L0_gnn_W, L0_ffn_ln1_g, L0_ffn_ln1_b, L0_ffn_w1, L0_ffn_b1, L0_ffn_ln2_g, L0_ffn_ln2_b, L0_ffn_w2, L0_ffn_b2, L1_gnn_W, L1_gnn_a_l, L1_gnn_a_r, L1_ffn_router_w, L1_ffn_router_b, L1_ffn_sw1, L1_ffn_sb1, L1_ffn_sw2, L1_ffn_sb2, L1_ffn_rw1, L1_ffn_rb1, L1_ffn_rw2, L1_ffn_rb2):
    import jax
    import jax.numpy as jnp

    def _L0_gnn_ref(x, W, edge_w, src, dst):
        import jax, jax.numpy as jnp
        import numpy as np
        N_NODES = 2500
        N_EDGES = 40000
        F_IN = 1024
        F_OUT = 1024
        support = jnp.matmul(x, W)
        messages = support[src] * edge_w[:, None]
        out = jax.ops.segment_sum(messages, dst, num_segments=N_NODES)
        return out

    def _L0_ffn_ref(x, ln1_g, ln1_b, w1, b1, ln2_g, ln2_b, w2, b2):
        import jax, jax.numpy as jnp
        import numpy as np
        LN_EPS = 1e-05

        def layer_norm(x, g, b):
            mu = jnp.mean(x, axis=-1, keepdims=True)
            var = jnp.mean(jnp.square(x - mu), axis=-1, keepdims=True)
            return (x - mu) * jax.lax.rsqrt(var + LN_EPS) * g + b

        def ternary_quant(w):
            scale = 1.0 / jnp.clip(jnp.mean(jnp.abs(w)), 1e-05)
            wq = jnp.clip(jnp.round(w * scale), -1.0, 1.0) / scale
            return w + jax.lax.stop_gradient(wq - w)
        h = layer_norm(x, ln1_g, ln1_b)
        h = jnp.einsum('bsd,hd->bsh', h, ternary_quant(w1)) + b1
        h = jax.nn.gelu(h, approximate=False)
        h = layer_norm(h, ln2_g, ln2_b)
        out = jnp.einsum('bsh,dh->bsd', h, ternary_quant(w2)) + b2
        return out

    def _L1_gnn_ref(h, W, a_l, a_r, src, dst):
        import jax, jax.numpy as jnp
        import numpy as np
        N, IN_FEAT, OUT_FEAT, HEADS, E = (2500, 1024, 256, 4, 40000)
        NEG_SLOPE = 0.2
        z = jnp.einsum('ni,hif->nhf', h, W)
        el = jnp.einsum('nhf,hf->nh', z, a_l)
        er = jnp.einsum('nhf,hf->nh', z, a_r)
        e = jax.nn.leaky_relu(el[src] + er[dst], NEG_SLOPE)
        m = jax.ops.segment_max(e, dst, num_segments=N)
        ex = jnp.exp(e - m[dst])
        s = jax.ops.segment_sum(ex, dst, num_segments=N)
        alpha = ex / s[dst]
        out = jax.ops.segment_sum(alpha[:, :, None] * z[src], dst, num_segments=N)
        return out.reshape(N, HEADS * OUT_FEAT)

    def _L1_ffn_ref(hidden, router_w, router_b, sw1, sb1, sw2, sb2, rw1, rb1, rw2, rb2):
        import jax, jax.numpy as jnp
        import numpy as np
        D = 1024
        H = 256
        E = 8
        TOP_K = 2
        N_SHARED = 1
        B, S = (2, 1024)
        b, s, d = hidden.shape
        T = b * s
        flat = hidden.reshape(T, d)
        router_logits = flat @ router_w + router_b
        router_probs = jax.nn.softmax(router_logits, axis=-1)
        topk_probs, topk_idx = jax.lax.top_k(router_probs, TOP_K)
        weights = jnp.zeros_like(router_probs).at[jnp.arange(T)[:, None], topk_idx].add(topk_probs)
        sh = jax.nn.gelu(flat @ sw1 + sb1, approximate=False)
        shared_out = (sh @ sw2 + sb2) / N_SHARED
        h1 = jax.nn.gelu(jnp.einsum('td,edh->teh', flat, rw1) + rb1[None], approximate=False)
        expert_out = jnp.einsum('teh,ehd->ted', h1, rw2) + rb2[None]
        mixed = jnp.einsum('ted,te->td', expert_out, weights)
        return (shared_out + mixed).reshape(b, s, d)
    x = x + _L0_gnn_ref(_layernorm(x, axis=-1), L0_gnn_W, edge_weight, src, dst)
    x = x + _L0_ffn_ref(_layernorm(x, axis=-1)[None], L0_ffn_ln1_g, L0_ffn_ln1_b, L0_ffn_w1, L0_ffn_b1, L0_ffn_ln2_g, L0_ffn_ln2_b, L0_ffn_w2, L0_ffn_b2)[0]
    x = x + _L1_gnn_ref(_layernorm(x, axis=-1), L1_gnn_W, L1_gnn_a_l, L1_gnn_a_r, src, dst)
    x = x + _L1_ffn_ref(_layernorm(x, axis=-1)[None], L1_ffn_router_w, L1_ffn_router_b, L1_ffn_sw1, L1_ffn_sb1, L1_ffn_sw2, L1_ffn_sb2, L1_ffn_rw1, L1_ffn_rb1, L1_ffn_rw2, L1_ffn_rb2)[0]
    return x

_drawn_inputs = setup_inputs


def setup_inputs(seed=0):
    import zlib

    import numpy as np

    out = dict(_drawn_inputs(seed))
    spreads = {'L0_ffn_ln1_g': (1.0, 0.2),
     'L0_ffn_ln1_b': (0.0, 0.476),
     'L0_ffn_b1': (0.0, 0.1),
     'L0_ffn_ln2_g': (1.0, 0.2),
     'L0_ffn_ln2_b': (0.0, 0.383),
     'L0_ffn_b2': (0.0, 0.1),
     'L1_ffn_router_b': (0.0, 0.8),
     'L1_ffn_sb1': (0.0, 0.729),
     'L1_ffn_sb2': (0.0, 0.1),
     'L1_ffn_rb1': (0.0, 0.8),
     'L1_ffn_rb2': (0.0, 0.422)}
    factors = {}
    for name, (base, spread) in spreads.items():
        noise = np.random.default_rng([zlib.crc32(name.encode()), seed]).standard_normal(out[name].shape)
        drawn = base * np.exp(spread * noise) if base else spread * noise
        out[name] = jnp.asarray(drawn.astype(out[name].dtype))
    for name, factor in factors.items():
        out[name] = (out[name] * factor).astype(out[name].dtype)
    return out
```

```python
from contextlib import ExitStack

import concourse.bass as bass
from concourse import mybir

F32 = mybir.dt.float32
F32R = mybir.dt.float32r
BF16 = mybir.dt.bfloat16
I32 = mybir.dt.int32
U32 = mybir.dt.uint32
ALU = mybir.AluOpType
ACT = mybir.ActivationFunctionType
AX = mybir.AxisListType

P = 128
N_NODES = 2500
N_EDGES = 40000
D = 1024
KD = D // P
HALF = 512
EPS = 1e-5
NT = -(-N_NODES // P)
LAST = N_NODES - (NT - 1) * P
NPAD = NT * P

EP, EC = 125, 320
GT = 2
NG = (N_EDGES + NT * (GT * P - 1)) // (GT * P)
NE = NG * GT
LISTS = 4

HID = 512
KH = HID // P
HEADS = 4
HF = D // HEADS
SLOPE = 0.2
BIG = 1e30

EXPERTS = 8
EH = 256
TOPK = 2
NPAIR = NT * TOPK
PG = (N_NODES * TOPK + EXPERTS * (GT * P - 1)) // (GT * P)
PG += PG % 2
PT = PG * GT


class Named(dict):
    __getattr__ = dict.__getitem__


class Steps:

    def __init__(self, eng, sem):
        self.eng, self.sem, self.n = eng, sem, 0

    def done(self, ins):
        ins.then_inc(self.sem, 1)
        self.n = self.n + 1

    def link(self, ins):
        self.done(ins)
        self.eng.wait_ge(self.sem, self.n)


def at_least(eng, sem, value):
    if not isinstance(value, int) or value > 0:
        eng.wait_ge(sem, value)


class Item:

    def __init__(self, j, unroll, off):
        self.j, self.unroll, self.off = j, unroll, off
        self.i = j * unroll + off

    def buf(self, count):
        return self.off % count

    def turn(self, count):
        return self.j * (self.unroll // count) + self.off // count


def in_steps(eng, count, unroll, body, steps=None, per_step=0, lead=1):
    turns = count // unroll
    assert turns * unroll == count

    def step(j, b, first, last):
        def item(lag):
            if (first and b < lag) or (last and b >= lag):
                return None
            return Item(j, unroll, b - lag)
        body(item, b)

    for j in range(lead):
        for b in range(unroll):
            step(j, b, j == 0, False)
    entry = steps.n if steps else 0
    with eng.Fori(lead, turns - 1) as j:
        if steps:
            steps.n = entry + (j - lead) * (unroll * per_step)
        for b in range(unroll):
            step(j, b, False, False)
    if steps:
        steps.n = entry + (turns - 1 - lead) * unroll * per_step
    for b in range(unroll):
        step(turns - 1, b, False, False)
    for b in range(unroll):
        step(turns, b, False, True)


class Alloc:

    def __init__(self, nc, ctx):
        self.nc, self.ctx, self.sems = nc, ctx, []
        ctx.callback(self.end)

    def end(self):
        if self.sems:
            self.nc.clear_and_free_semaphores(self.sems)
            self.nc.all_engine_barrier()

    def sb(self, name, shape, dt=F32):
        return self.ctx.enter_context(self.nc.sbuf_tensor(name, shape, dt))

    def psum(self, name, shape, dt=F32):
        return self.ctx.enter_context(self.nc.psum_tensor(name, shape, dt))

    def sem(self, name):
        self.sems.append(self.nc.alloc_semaphore(name))
        return self.sems[-1]



def projection_tiles(a, name, x_ring, zout=True):
    n = name
    r = Named(
        name=n,
        stats=a.sb(f"{n}_stats", [P, 2, 2, 6]), mv=a.sb(f"{n}_mv", [P, 2, 2]),
        std=a.sb(f"{n}_std", [P, 2]), rstd=a.sb(f"{n}_rstd", [P, 2]), nmr=a.sb(f"{n}_nmr", [P, 2]),
        xn=a.sb(f"{n}_xn", [P, 2, D]),
        hi=a.sb(f"{n}_hi", [P, 2, KD, P], F32R), lo=a.sb(f"{n}_lo", [P, 2, KD, P], F32R),
        zout=a.sb(f"{n}_zout", [P, 2, D]),
        turned=a.psum(f"{n}_turned", [P, 2, HALF]), z=a.psum(f"{n}_z", [P, 2, 2, HALF]),
        x_ring=a.sb(f"{n}_x", [P, 2, D]) if x_ring else None,
        x_in=[a.sem(f"{n}_x_in{b}") for b in range(2)],
        stored=[a.sem(f"{n}_stored{b}") for b in range(2)],
        **{s: a.sem(f"{n}_{s}") for s in ("mv_ready", "std_ready", "rstd_ready", "xn_ready", "turned_ready",
                                          "hi_ready", "lo_ready", "z_ready", "out_v", "out_a")},
    )
    return r


def projection_vector(nc, dve, r, st, x_of, x_wait, extra=None):
    v = nc.vector

    def body(item, b):
        it = item(0)
        if it:
            k = it.buf(2)
            x_wait(dve, it)
            at_least(dve, r.xn_ready, it.i - 1)
            st.done(v.bn_stats(r.stats[:, k, 0, :], x_of(it)[:, 0:HALF]))
            st.link(v.bn_stats(r.stats[:, k, 1, :], x_of(it)[:, HALF:D]))
            dve.sem_inc(r.pace, 1)
            v.bn_aggr(r.mv[:, k, :], r.stats[:, k, :, :]).then_inc(r.mv_ready, 1)
        it = item(1)
        if it:
            k = it.buf(2)
            dve.wait_ge(r.hi_ready, it.i + 1)
            v.tensor_tensor(r.lo[:, k].rearrange("p k n -> p (k n)"),
                            r.turned[:].rearrange("p h n -> p (h n)"),
                            r.hi[:, k].bitcast(F32).rearrange("p k n -> p (k n)"),
                            ALU.subtract).then_inc(r.lo_ready, 1)
        it = item(0)
        if it:
            k = it.buf(2)
            dve.wait_ge(r.std_ready, it.i + 1)
            st.link(v.reciprocal(r.rstd[:, k:k + 1], r.std[:, k:k + 1]))
            v.scalar_tensor_tensor(out=r.nmr[:, k:k + 1], in0=r.mv[:, k, 0:1], scalar=-1.0,
                                   in1=r.rstd[:, k:k + 1], op0=ALU.mult, op1=ALU.mult).then_inc(r.rstd_ready, 1)
        it = item(3)
        if it:
            k = it.buf(2)
            dve.wait_ge(r.z_ready, it.i + 1)
            at_least(dve, r.stored[k], it.turn(2) * 16)
            if extra:
                extra(it)
            v.tensor_copy(r.zout[:, k, 0:HALF], r.z[:, k, 0, :]).then_inc(r.out_v, 1)

    in_steps(dve, NT, 4, body, st, 3)


def projection_scalar(nc, act, r, x_of, x_wait, eps):
    s = nc.scalar

    def body(item, b):
        it = item(0)
        if it:
            k = it.buf(2)
            act.wait_ge(r.mv_ready, it.i + 1)
            s.activation(r.std[:, k:k + 1], r.mv[:, k, 1:2], ACT.Sqrt, bias=eps[:, 0:1]).then_inc(r.std_ready, 1)
        it = item(1)
        if it:
            k = it.buf(2)
            act.wait_ge(r.turned_ready, it.i + 1)
            at_least(act, r.z_ready, it.i - 1)
            s.copy(r.hi[:, k].rearrange("p k n -> p (k n)"),
                   r.turned[:].rearrange("p h n -> p (h n)")).then_inc(r.hi_ready, 1)
        it = item(0)
        if it:
            k = it.buf(2)
            x_wait(act, it)
            at_least(act, r.turned_ready, it.i - 1)
            act.wait_ge(r.rstd_ready, it.i + 1)
            act.sem_inc(r.pace, 1)
            s.activation(r.xn[:, k, :], x_of(it), ACT.Identity, bias=r.nmr[:, k:k + 1],
                         scale=r.rstd[:, k:k + 1]).then_inc(r.xn_ready, 1)
        it = item(3)
        if it:
            k = it.buf(2)
            act.wait_ge(r.z_ready, it.i + 1)
            at_least(act, r.stored[k], it.turn(2) * 16)
            s.copy(r.zout[:, k, HALF:D], r.z[:, k, 1, :]).then_inc(r.out_a, 1)

    in_steps(act, NT, 4, body)


def split_products(pe, out, lefts, rights, chunks, start=True, stop=True):
    for k in range(chunks):
        (lh, ll), (rh, rl) = lefts(k), rights(k)
        for n, (x, y) in enumerate(((lh, rh), (lh, rl), (ll, rh))):
            mm = pe.matmul(out, x, y, start=start and k == 0 and n == 0, stop=stop and k == chunks - 1 and n == 2)
    return mm


def projection_tensor(nc, pe, r, w_hi, w_lo, ident, extra=None):
    t = nc.tensor

    def body(item, b):
        it = item(1)
        if it:
            k = it.buf(2)
            pe.wait_ge(r.xn_ready, it.i + 1)
            at_least(pe, r.lo_ready, it.i)
            for c in range(KD):
                tr = t.transpose(r.turned[:, c // 4, (c % 4) * P:(c % 4 + 1) * P],
                                 r.xn[:, k, c * P:(c + 1) * P], ident[:])
            tr.then_inc(r.turned_ready, 1)
        it = item(2)
        if it:
            k = it.buf(2)
            pe.wait_ge(r.lo_ready, it.i + 1)
            pe.wait_ge(r.hi_ready, it.i + 1)
            at_least(pe, r.out_v, it.i - 1)
            at_least(pe, r.out_a, it.i - 1)
            if extra:
                extra(it)
            for h in range(2):
                mm = split_products(t, r.z[:, k, h, :], lambda c: (r.hi[:, k, c, :], r.lo[:, k, c, :]),
                                    lambda c: (w_hi[:, c, h * HALF:(h + 1) * HALF], w_lo[:, c, h * HALF:(h + 1) * HALF]), KD)
            mm.then_inc(r.z_ready, 1)

    in_steps(pe, NT, 4, body)


def projection_sync(sp, r, x, z_dram, load=True):
    def load_rows(it):
        k = it.buf(2)
        rows = LAST if isinstance(it.i, int) and it.i == NT - 1 else P
        at_least(sp, r.xn_ready, it.i - 1)
        sp.dma_start(r.x_ring[0:rows, k, :], x[bass.ds(it.i * P, rows), :]).then_inc(r.x_in[k], 16)

    def body(item, b):
        it = item(0)
        if it and load:
            load_rows(it)
        it = item(3)
        if it:
            k = it.buf(2)
            sp.wait_ge(r.out_v, it.i + 1)
            sp.wait_ge(r.out_a, it.i + 1)
            sp.dma_start(z_dram[bass.ds(it.i * P, P), :], r.zout[:, k, :]).then_inc(r.stored[k], 16)

    in_steps(sp, NT, 4, body)
    for k in range(2):
        sp.wait_ge(r.stored[k], 16 * (NT // 2))



def sort_tiles(a, name, cols, buckets, groups):
    sb = lambda n, s, dt=F32: a.sb(f"{name}_{n}", s, dt)
    return Named(
        bucket=sb("bucket", [P, cols]), in_bucket=sb("in_bucket", [P, cols], BF16),
        earlier=sb("earlier", [P, P], BF16), ones=sb("ones", [P, P], BF16),
        iota_b=sb("iota_b", [P, buckets]), iota_g=sb("iota_g", [P, groups]), none=sb("none", [P, cols]),
        cum=sb("cum", [P, cols]), chosen=sb("chosen", [P, cols]), place=sb("place", [P, cols]),
        base=sb("base", [P, buckets + 1]), base_i=sb("base_i", [P, 2], I32), of_group=sb("of_group", [P, groups]),
        counts=a.psum(f"{name}_counts", [P, 2, HALF]),
        bucket_ready=a.sem(f"{name}_bucket_ready"), counted=a.sem(f"{name}_counted"))


def sort_constants(nc, pool, o, cols, buckets, groups, ready, before):
    q = nc.gpsimd
    q.memset(o.ones[:], 1.0)
    q.memset(o.none[:], 0.0)
    q.memset(o.earlier[:], 0.0).then_inc(ready, 1)
    pool.wait_ge(ready, before + 1)
    q.affine_select(out=o.earlier[:], in_=o.earlier[:], compare_op=ALU.is_gt, fill=-1.0, base=0,
                    pattern=[[1, P]], channel_multiplier=-1)
    q.iota(o.iota_b[:], pattern=[[1, buckets]], base=0, channel_multiplier=0, allow_small_or_imprecise_dtypes=True)
    q.iota(o.iota_g[:], pattern=[[GT * P, groups]], base=0, channel_multiplier=0,
           allow_small_or_imprecise_dtypes=True).then_inc(ready, 1)


def sort_tensor(nc, pe, o, rows, cols, buckets):
    with pe.Fori(0, buckets) as b:
        pe.wait_ge(o.bucket_ready, b + 1)
        nc.tensor.matmul(o.counts[:, 0, 0:cols], o.ones[rows, :], o.in_bucket[rows, :], start=True, stop=True)
        nc.tensor.matmul(o.counts[:, 1, 0:cols], o.earlier[rows, :], o.in_bucket[rows, :], start=True,
                         stop=True).then_inc(o.counted, 1)


def sort_vector(nc, dve, st, o, rows, cols, buckets):
    v = nc.vector
    v.memset(o.base[:, 0:1], 0.0)
    v.memset(o.of_group[:], 0.0)
    st.link(v.memset(o.place[:], 0.0))
    first, per = st.n, 8
    with dve.Fori(0, buckets) as b:
        st.n = b * per + first
        v.tensor_scalar(o.in_bucket[rows], o.bucket[rows], o.iota_b[rows, bass.ds(b, 1)], None,
                        ALU.is_equal).then_inc(o.bucket_ready, 1)
        dve.wait_ge(o.counted, b + 1)
        st.link(v.tensor_tensor_scan(o.cum[:], o.counts[:, 0, 0:cols], o.none[:], o.base[:, bass.ds(b, 1)],
                                     ALU.add, ALU.add))
        st.done(v.tensor_scalar(o.base_i[:, 0:1], o.cum[:, cols - 1:cols], float(GT * P - 1), None, ALU.add))
        st.link(v.tensor_tensor(o.chosen[:], o.cum[:], o.counts[:, 1, 0:cols], ALU.add))
        st.link(v.tensor_scalar(o.base_i[:, 1:2], o.base_i[:, 0:1], -GT * P, None, ALU.bitwise_and))
        st.done(v.tensor_copy(o.base[:, bass.ds(b + 1, 1)], o.base_i[:, 1:2]))
        st.link(v.tensor_tensor(o.chosen[rows], o.chosen[rows], o.in_bucket[rows], ALU.mult))
        st.link(v.tensor_tensor(o.place[rows], o.place[rows], o.chosen[rows], ALU.add))
        st.link(v.scalar_tensor_tensor(out=o.of_group[:], in0=o.iota_g[:], scalar=o.base[:, bass.ds(b + 1, 1)],
                                       in1=o.of_group[:], op0=ALU.is_ge, op1=ALU.add))
    st.n = first + per * buckets



def weight_chunks_sync(sp, chunks, raw, raw_in, raw_used, first=0):
    for n, chunk in enumerate(chunks, first):
        at_least(sp, raw_used, n - 1)
        view = raw[:, n % 2, :]
        if len(chunk.shape) == 3:
            view = view.rearrange("p (a b) -> p a b", a=chunk.shape[1])
        sp.dma_start(view, chunk).then_inc(raw_in[n % 2], 16)


def stage_sort_and_project(nc, g):
    with ExitStack() as ctx:
        a = Alloc(nc, ctx)
        sb, sem = a.sb, a.sem
        r = projection_tiles(a, "z0", True)
        r.pace = sem("z0_pace")
        w_hi, w_lo = sb("w0_hi", [P, KD, D], F32R), sb("w0_lo", [P, KD, D], F32R)
        raw = sb("raw", [P, 2, D])
        dst_i, bucket_i = sb("dst_i", [P, EC], I32), sb("bucket_i", [P, EC], I32)
        src_in, w_in = sb("src_in", [P, EC], I32), sb("w_in", [P, EC])
        o = sort_tiles(a, "esort", EC, NT, NG)
        payload = sb("payload", [P, EC, 4])
        place_i, col_i, row_i = (sb(n, [P, EC], I32) for n in ("place_i", "col_i", "row_i"))
        zero, merged = sb("zero", [P, NE * 4]), sb("merged", [P, 3, NE, 4])
        staged_row, staged_pay = sb("staged_row", [P, 2, LISTS], I32), sb("staged_pay", [P, 2, LISTS, 4])
        att = sb("att", [P, 2, D])
        att_prod = sb("att_prod", [P, D])
        att_w = sb("att_w", [P, KD, 8])
        abs_sum, abs_all = sb("abs_sum", [P, 2, 4]), sb("abs_all", [P, 2])
        cut, quant = sb("cut", [P, D]), sb("quant", [P, D])
        ones_f = sb("ones_f", [P, P])

        edges_in, att_in = sem("edges_in"), sem("att_in")
        raw_in, raw_used = [sem(f"raw_in{k}") for k in range(2)], sem("raw_used")
        w_split = sem("w_split")
        zeros_ready, lists_clear, pool_ready = sem("zeros_ready"), sem("lists_clear"), sem("pool_ready")
        rows_ready = sem("rows_ready")
        staged, merge_used = sem("staged"), sem("merge_used")
        scattered = [sem(f"scattered{k}") for k in range(LISTS)]
        merged_in = [sem(f"merged_in{k}") for k in range(LISTS)]
        scatter_pace, v_done = sem("scatter_pace"), sem("v_done")
        abs_ready, sums_ready, quant_ready, quant_turned, quant_kept = (
            sem(n) for n in ("abs_ready", "sums_ready", "quant_ready", "quant_turned", "quant_kept"))

        w1_rows = g.w1.rearrange("(m p) d -> m p d", p=P)
        w2_rows = g.w2.rearrange("(m a p) h -> m p a h", p=P, a=2)
        w0_rows = g.W0.rearrange("(c p) n -> c p n", p=P)
        watt_rows = g.W1.rearrange("h (c p) f -> c p h f", p=P)
        quant_chunks = [w1_rows[m] for m in range(4)] + [w2_rows[m] for m in range(4)]
        W_CHUNKS = KD
        chunks = ([w0_rows[c] for c in range(KD)] + quant_chunks + quant_chunks
                  + [watt_rows[c] for c in range(KD)])

        block = ctx.enter_context(nc.Block())

        @block.sync
        def _(sp):
            rows = lambda t: t.rearrange("(p c) -> p c", p=EP)
            sp.dma_start(dst_i[0:EP, :], rows(g.dst)).then_inc(edges_in, 16)
            sp.dma_start(src_in[0:EP, :], rows(g.src_in)).then_inc(edges_in, 16)
            sp.dma_start(w_in[0:EP, :], rows(g.edge_weight)).then_inc(edges_in, 16)
            sp.wait_ge(zeros_ready, 1)
            for k in range(LISTS):
                sp.dma_start(g.lists[k].rearrange("(p t) k -> p (t k)", p=P), zero[:]).then_inc(lists_clear, 16)
            weight_chunks_sync(sp, chunks[0:W_CHUNKS], raw, raw_in, raw_used)
            projection_sync(sp, r, g.x, g.z0)
            for n, vector in enumerate((g.a_l, g.a_r)):
                sp.dma_start(att[:, n, :], vector.rearrange("h f -> (h f)").partition_broadcast(P)).then_inc(att_in, 16)
            weight_chunks_sync(sp, chunks[W_CHUNKS:], raw, raw_in, raw_used, W_CHUNKS)
            for k in range(LISTS):
                sp.wait_ge(scattered[k], 16 * (EC // LISTS))
                if k == 3:
                    sp.wait_ge(merge_used, 1)
                sp.dma_start(merged[:, (0, 1, 2, 1)[k]], g.lists[k].rearrange("(p t) k -> p t k", p=P)).then_inc(merged_in[k], 16)

        @block.gpsimd
        def _(pool):
            q = nc.gpsimd
            q.memset(zero[:], 0.0).then_inc(zeros_ready, 1)
            q.memset(ones_f[:], 1.0)
            q.memset(g.eps[:], EPS)
            q.memset(g.ident[:], 0.0).then_inc(pool_ready, 1)
            pool.wait_ge(pool_ready, 1)
            q.affine_select(out=g.ident[:], in_=g.ident[:], compare_op=ALU.not_equal, fill=1.0, base=0,
                            pattern=[[-1, P]], channel_multiplier=1)
            q.iota(g.iota1[:], pattern=[[1, P]], base=1, channel_multiplier=0,
                   allow_small_or_imprecise_dtypes=True)
            sort_constants(nc, pool, o, EC, NT, NG, pool_ready, 1)
            pool.wait_ge(lists_clear, 16 * LISTS)
            pool.wait_ge(rows_ready, 1)

            def scatter_columns(i):
                for half in range(2):
                    turn = i * 2 + half
                    cols = bass.ds(turn * LISTS, LISTS)
                    q.tensor_copy(staged_row[0:EP, half, :], row_i[0:EP, cols])
                    q.tensor_copy(staged_pay[0:EP, half, :, :], payload[0:EP, cols, :]).then_inc(staged, 1)
                    pool.wait_ge(staged, turn + 1)
                    for k in range(LISTS):
                        at_least(pool, scattered[k], turn * 16)
                        pool.sem_inc(scatter_pace, 1)
                        pool.indirect_dma_start(
                            out=g.lists[k],
                            out_offset=bass.IndirectOffsetOnAxis(ap=staged_row[0:EP, half, k:k + 1], axis=0),
                            in_=staged_pay[0:EP, half, k, :], in_offset=None).then_inc(scattered[k], 16)

            scatter_columns(0)
            with pool.Fori(1, EC // LISTS // 2) as i:
                scatter_columns(i)

        @block.tensor
        def _(pe):
            pe.wait_ge(pool_ready, 3)
            sort_tensor(nc, pe, o, slice(0, EP), EC, NT)
            pe.wait_ge(w_split, KD)
            pe.wait_ge(raw_used, KD)
            projection_tensor(nc, pe, r, w_hi, w_lo, g.ident)
            pe.wait_ge(abs_ready, 1)
            nc.tensor.matmul(o.counts[:, 0, 0:2], ones_f[:], abs_all[:], start=True, stop=True).then_inc(sums_ready, 1)
            for m in range(8):
                pe.wait_ge(quant_ready, m + 1)
                if m:
                    pe.wait_ge(quant_kept, m)
                for c in range(8):
                    tr = nc.tensor.transpose(r.turned[:, c // 4, (c % 4) * P:(c % 4 + 1) * P],
                                             quant[:, c * P:(c + 1) * P], g.ident[:])
                tr.then_inc(quant_turned, 1)

        @block.scalar
        def _(act):
            s = nc.scalar
            act.wait_ge(pool_ready, 3)
            for c in range(KD):
                act.wait_ge(raw_in[c % 2], 16 * (c // 2 + 1))
                s.copy(w_hi[:, c, :], raw[:, c % 2, :]).then_inc(w_split, 1)
            projection_scalar(nc, act, r, lambda it: r.x_ring[:, it.buf(2), :],
                              lambda e, it: e.wait_ge(r.x_in[it.buf(2)], (it.turn(2) + 1) * 16), g.eps)
            for m in range(8):
                act.wait_ge(quant_turned, m + 1)
                if m < 4:
                    out = g.t1[:, :, m * P:(m + 1) * P]
                    src = r.turned[:].rearrange("p h (c n) -> p (h c) n", n=P)
                else:
                    out = g.t2[:, :, (m - 4) * 2 * P:(m - 3) * 2 * P].rearrange("p c (a n) -> p a c n", a=2)
                    src = r.turned[:].rearrange("p a (c n) -> p a c n", n=P)
                s.copy(out, src).then_inc(quant_kept, 1)

        @block.vector
        def _(dve):
            v = nc.vector
            st = Steps(dve, v_done)
            dve.wait_ge(edges_in, 48)
            dve.wait_ge(pool_ready, 3)
            dve.wait_ge(zeros_ready, 1)
            e = slice(0, EP)
            v.memset(payload[:, :, 3], 0.0)
            v.tensor_copy(payload[e, :, 2], w_in[e])
            v.tensor_copy(payload[e, :, 0], src_in[e])
            st.link(v.tensor_scalar(bucket_i[e], dst_i[e], 7, None, ALU.arith_shift_right))
            st.done(v.tensor_copy(o.bucket[e], bucket_i[e]))
            st.link(v.tensor_copy(payload[e, :, 1], dst_i[e]))
            st.link(v.scalar_tensor_tensor(out=payload[e, :, 1], in0=o.bucket[e], scalar=-float(P),
                                           in1=payload[e, :, 1], op0=ALU.mult, op1=ALU.add))
            st.link(v.tensor_scalar(payload[e, :, 1], payload[e, :, 1], 1.0, None, ALU.add))
            sort_vector(nc, dve, st, o, e, EC, NT)
            st.link(v.tensor_copy(place_i[e], o.place[e]))
            st.done(v.tensor_scalar(col_i[e], place_i[e], 7, None, ALU.arith_shift_right))
            st.link(v.tensor_scalar(row_i[e], place_i[e], P - 1, None, ALU.bitwise_and))
            v.scalar_tensor_tensor(out=row_i[e], in0=row_i[e], scalar=float(NE), in1=col_i[e], op0=ALU.mult,
                                   op1=ALU.add).then_inc(rows_ready, 1)
            st.link(v.tensor_scalar(g.ntile[:], o.of_group[:], float(NT - 1), None, ALU.min))
            for c in range(KD):
                dve.wait_ge(raw_in[c % 2], 16 * (c // 2 + 1))
                dve.wait_ge(w_split, c + 1)
                v.tensor_tensor(w_lo[:, c, :], raw[:, c % 2, :], w_hi[:, c, :].bitcast(F32),
                                ALU.subtract).then_inc(raw_used, 1)
            projection_vector(nc, dve, r, st, lambda it: r.x_ring[:, it.buf(2), :],
                              lambda e, it: e.wait_ge(r.x_in[it.buf(2)], (it.turn(2) + 1) * 16))

            def arrived(n):
                dve.wait_ge(raw_in[n % 2], 16 * (n // 2 + 1))
            for m in range(8):
                arrived(KD + m)
                v.tensor_reduce(abs_sum[:, m // 4, m % 4:m % 4 + 1], raw[:, m % 2, :], AX.X, ALU.add,
                                apply_absolute_value=True).then_inc(raw_used, 1)
            dve.wait_ge(raw_used, KD + 8)
            v.tensor_reduce(abs_all[:], abs_sum[:], AX.X, ALU.add).then_inc(abs_ready, 1)
            dve.wait_ge(sums_ready, 1)
            st.link(v.tensor_scalar(g.unit[:], o.counts[:, 0, 0:2], 1.0 / (HID * D), 1e-5, ALU.mult, ALU.max))
            st.link(v.reciprocal(g.scale[:], g.unit[:]))
            for m in range(8):
                n = KD + 8 + m
                arrived(n)
                sc = g.scale[:, m // 4:m // 4 + 1]
                v.tensor_scalar(cut[:], raw[:, n % 2, :], sc, -0.5, ALU.mult, ALU.is_lt)
                if m:
                    dve.wait_ge(quant_turned, m)
                v.tensor_scalar(quant[:], raw[:, n % 2, :], sc, 0.5, ALU.mult, ALU.is_gt).then_inc(raw_used, 1)
                dve.wait_ge(raw_used, n + 1)
                v.tensor_tensor(quant[:], quant[:], cut[:], ALU.subtract).then_inc(quant_ready, 1)
                dve.wait_ge(quant_ready, m + 1)
            dve.wait_ge(att_in, 32)
            for c in range(KD):
                n = KD + 16 + c
                arrived(n)
                for side in range(2):
                    ins = v.tensor_tensor(att_prod[:], raw[:, n % 2, :], att[:, side, :], ALU.mult)
                    if side:
                        ins.then_inc(raw_used, 1)
                        dve.wait_ge(raw_used, n + 1)
                    else:
                        st.link(ins)
                    st.link(v.tensor_reduce(att_w[:, c, side * HEADS:(side + 1) * HEADS],
                                            att_prod[:].rearrange("p (h f) -> p h f", h=HEADS), AX.X, ALU.add))
            st.link(v.tensor_copy(g.att_hi[:], att_w[:]))
            st.link(v.tensor_tensor(g.att_lo[:], att_w[:], g.att_hi[:].bitcast(F32), ALU.subtract))
            dve.wait_ge(merged_in[0], 16)
            total = merged[:, 0].rearrange("p t k -> p (t k)")
            for k in range(1, LISTS):
                dve.wait_ge(merged_in[k], 16)
                v.tensor_tensor(total, total, merged[:, (0, 1, 2, 1)[k]].rearrange("p t k -> p (t k)"),
                                ALU.add).then_inc(merge_used, 1)
                dve.wait_ge(merge_used, k)
            v.tensor_copy(g.src[:], merged[:, 0, :, 0])
            v.tensor_copy(g.place[:], merged[:, 0, :, 1])
            v.tensor_copy(g.weight[:], merged[:, 0, :, 2])



def gather_groups(nc, pool, r, g, table):
    def body(item, b):
        it = item(0)
        if it:
            at_least(pool, r.multiplied, it.i - 3)
            nc.gpsimd.tensor_copy(r.staged[:, it.buf(4), :], g.src[:, bass.ds(it.i * GT, GT)]).then_inc(r.staged_ready, 1)
            pool.wait_ge(r.staged_ready, it.i + 1)
            pool.sem_inc(r.pace, 1)
            for q in range(GT):
                slot = it.buf(4) * GT + q
                pool.indirect_dma_start(
                    out=r.rows[:, slot, :], out_offset=None, in_=table,
                    in_offset=bass.IndirectOffsetOnAxis(ap=r.staged[:, it.buf(4), q:q + 1], axis=0),
                ).then_inc(r.gathered[slot], 16)

    in_steps(pool, NG, 4, body)


def stage_first_graph(nc, g):
    with ExitStack() as ctx:
        a = Alloc(nc, ctx)
        r = Named(
            rows=a.sb("g0_rows", [P, 4 * GT, D]), staged=a.sb("g0_staged", [P, 4, GT], I32),
            gathered=[a.sem(f"g0_gathered{k}") for k in range(4 * GT)],
            **{s: a.sem(f"g0_{s}") for s in ("staged_ready", "multiplied", "pace")})
        share = a.sb("g0_share", [P, 4, P])
        goes = a.sb("g0_goes", [P, 4, P], F32R)
        scaled_hi, scaled_lo = a.sb("g0_scaled_hi", [P, 2, D], F32R), a.sb("g0_scaled_lo", [P, 2, D], F32R)
        sums = a.psum("g0_sums", [P, 4, 2, HALF])
        pads_ready, x_in = a.sem("g0_pads_ready"), [a.sem("g0_x_in0"), a.sem("g0_x_in1")]
        share_ready, added, scaled_ready, split_ready = (
            a.sem(f"g0_{n}") for n in ("share_ready", "added", "scaled_ready", "split_ready"))
        x_flat = g.x_all[:].rearrange("p t d -> p (t d)")

        block = ctx.enter_context(nc.Block())

        @block.sync
        def _(sp):
            full = (NT - 1) * P
            sp.dma_start(g.x_all[:, 0:NT - 1, :], g.x[0:full, :].rearrange("(t p) d -> p t d", p=P)).then_inc(x_in[0], 16)
            sp.wait_ge(pads_ready, 1)
            sp.dma_start(g.x_all[0:LAST, NT - 1, :], g.x[full:N_NODES, :]).then_inc(x_in[1], 16)

        @block.gpsimd
        def _(pool):
            nc.gpsimd.memset(g.x_all[LAST // 32 * 32:P, NT - 1, :], 0.0).then_inc(pads_ready, 1)
            pool.wait_ge(pads_ready, 1)
            gather_groups(nc, pool, r, g, g.z0)

        @block.scalar
        def _(act):
            s = nc.scalar

            def body(item, b):
                it = item(2)
                if it:
                    k, m = it.buf(4), it.buf(2)
                    act.wait_ge(r.gathered[k * GT + 1], (it.turn(4) + 1) * 16)
                    at_least(act, r.multiplied, it.i - 1)
                    act.sem_inc(r.pace, 1)
                    s.activation(scaled_hi[:, m, :], r.rows[:, k * GT + 1, :], ACT.Copy,
                                 scale=g.weight[:, bass.ds(it.i * GT + 1, 1)]).then_inc(scaled_ready, 1)
            in_steps(act, NG, 4, body, lead=2)

        @block.tensor
        def _(pe):
            def body(item, b):
                it = item(3)
                if it:
                    k, m = it.buf(4), it.buf(2)
                    pe.wait_ge(share_ready, it.i + 1)
                    at_least(pe, added, it.i - 3)
                    pe.wait_ge(r.gathered[k * GT], (it.turn(4) + 1) * 16)
                    for h in range(2):
                        nc.tensor.matmul(sums[:, k, h, :], share[:, k, :],
                                         r.rows[:, k * GT, h * HALF:(h + 1) * HALF], start=True, stop=False)
                    pe.wait_ge(split_ready, it.i + 1)
                    for h in range(2):
                        for n, part in enumerate((scaled_hi, scaled_lo)):
                            mm = nc.tensor.matmul(sums[:, k, h, :], goes[:, k, :],
                                                  part[:, m, h * HALF:(h + 1) * HALF], start=False, stop=n == 1)
                    mm.then_inc(r.multiplied, 1)
            in_steps(pe, NG, 4, body, lead=2)

        @block.vector
        def _(dve):
            v = nc.vector
            dve.wait_ge(x_in[0], 16)
            dve.wait_ge(x_in[1], 16)

            def body(item, b):
                it = item(2)
                if it:
                    k, m = it.buf(4), it.buf(2)
                    dve.wait_ge(scaled_ready, it.i + 1)
                    at_least(dve, r.multiplied, it.i - 1)
                    dve.sem_inc(r.pace, 1)
                    v.scalar_tensor_tensor(out=scaled_lo[:, m, :], in0=r.rows[:, k * GT + 1, :],
                                           scalar=g.weight[:, bass.ds(it.i * GT + 1, 1)],
                                           in1=scaled_hi[:, m, :].bitcast(F32), op0=ALU.mult,
                                           op1=ALU.subtract).then_inc(split_ready, 1)
                it = item(4)
                if it:
                    tile = dve.value_load(g.ntile[0:1, bass.ds(it.i, 1)], min_val=0, max_val=NT - 1)
                    to = x_flat[:, bass.ds(tile * D, D)]
                    dve.wait_ge(r.multiplied, it.i + 1)
                    at_least(dve, added, it.i)
                    v.tensor_tensor(to, to, sums[:, it.buf(4)].rearrange("p h n -> p (h n)"), ALU.add).then_inc(added, 1)
                it = item(0)
                if it:
                    k = it.buf(4)
                    at_least(dve, r.multiplied, it.i - 3)
                    dve.sem_inc(r.pace, 1)
                    v.tensor_scalar(share[:, k, :], g.iota1[:], g.place[:, bass.ds(it.i * GT, 1)],
                                    g.weight[:, bass.ds(it.i * GT, 1)], ALU.is_equal, ALU.mult)
                    v.tensor_scalar(goes[:, k, :], g.iota1[:], g.place[:, bass.ds(it.i * GT + 1, 1)], None,
                                    ALU.is_equal).then_inc(share_ready, 1)

            in_steps(dve, NG, 4, body, lead=2)



def stage_first_ffn(nc, g):
    with ExitStack() as ctx:
        a = Alloc(nc, ctx)
        sb = lambda n, s, dt=F32: a.sb(f"f0_{n}", s, dt)
        sem = lambda n: a.sem(f"f0_{n}")
        t1, t2 = sb("t1", [P, KD, HID], F32R), sb("t2", [P, KH, D], F32R)
        gain1, shift1 = sb("gain1", [P, KD]), sb("shift1", [P, KD])
        gain2, shift2 = sb("gain2", [P, KH]), sb("shift2", [P, KH])
        b1, b2 = sb("b1", [P, HID]), sb("b2", [P, D])
        eps_eps = sb("eps_eps", [P, 1])
        stats, mv = sb("stats", [P, 2, 2, 6]), sb("mv", [P, 2, 2])
        std, rstd, nmr = (sb(n, [P, 2]) for n in ("std", "rstd", "nmr"))
        rows, cols = sb("rows", [P, 2, D]), sb("cols", [P, KD, P])
        hi, lo = sb("hi", [P, 2, KD, P], F32R), sb("lo", [P, 2, KD, P], F32R)
        pre, hidden = sb("pre", [P, 2, HID]), sb("hidden", [P, 2, HID])
        stats2, mv2, std2, rstd2 = sb("stats2", [P, 6]), sb("mv2", [P, 2]), sb("std2", [P, 1]), sb("rstd2", [P, 1])
        rows2, cols2 = sb("rows2", [P, HID]), sb("cols2", [P, KH, P])
        hi2, lo2 = sb("hi2", [P, 2, KH, P], F32R), sb("lo2", [P, 2, KH, P], F32R)
        turned, turned2 = a.psum("f0_turned", [P, 2, HALF]), a.psum("f0_turned2", [P, HALF])
        h1, h2 = a.psum("f0_h1", [P, 2, HID]), a.psum("f0_h2", [P, 2, HALF])
        x_flat = g.x_all[:].rearrange("p t d -> p (t d)")

        (small_in, weights_ready, mv_ready, std_ready, rstd_ready, rows_ready, turned_ready, cols_ready, split_ready,
         h1_ready, pre_ready, hidden_ready, mv2_ready, std2_ready, rows2_ready, turned2_ready, cols2_ready,
         split2_ready, h2_ready, shifted, x_ready, stored, v_done, pace) = (sem(n) for n in (
             "small_in", "weights_ready", "mv_ready", "std_ready", "rstd_ready", "rows_ready", "turned_ready",
             "cols_ready", "split_ready", "h1_ready", "pre_ready", "hidden_ready", "mv2_ready", "std2_ready",
             "rows2_ready", "turned2_ready", "cols2_ready", "split2_ready", "h2_ready", "shifted", "x_ready",
             "stored", "v_done", "pace"))

        def x_tile(it):
            return x_flat[:, bass.ds(it.i * D, D)]

        block = ctx.enter_context(nc.Block())

        @block.sync
        def _(sp):
            with nc.allow_non_contiguous_dma(reason="a few thousand parameters"):
                for tile, vector in ((gain1, g.ln1_g), (shift1, g.ln1_b), (gain2, g.ln2_g), (shift2, g.ln2_b)):
                    sp.dma_start(tile[:], vector.rearrange("(c p) -> p c", p=P)).then_inc(small_in, 16)
            sp.dma_start(b1[:], g.b1.partition_broadcast(P)).then_inc(small_in, 16)
            sp.dma_start(b2[:], g.b2.partition_broadcast(P)).then_inc(small_in, 16)

            def body(item, b):
                it = item(4)
                if it:
                    sp.wait_ge(x_ready, it.i + 1)
                    sp.dma_start(g.x2[bass.ds(it.i * P, P), :], x_tile(it)).then_inc(stored, 16)
            in_steps(sp, NT, 4, body, lead=2)
            sp.wait_ge(stored, 16 * NT)

        @block.gpsimd
        def _(pool):
            nc.gpsimd.tensor_copy(t2[:].rearrange("p c n -> p (c n)"),
                                  g.t2[:].rearrange("p c n -> p (c n)")).then_inc(weights_ready, 1)
            pool.wait_ge(small_in, 96)

            def body(item, b):
                it = item(0)
                if it:
                    pool.wait_ge(rows_ready, it.i + 1)
                    pool.sem_inc(pace, 1)
                    nc.gpsimd.tensor_tensor(x_tile(it), x_tile(it), b2[:], ALU.add).then_inc(shifted, 1)
            in_steps(pool, NT, 4, body, lead=2)

        @block.tensor
        def _(pe):
            t = nc.tensor
            pe.wait_ge(weights_ready, 2)

            def body(item, b):
                it = item(1)
                if it:
                    k = it.buf(2)
                    pe.wait_ge(rows_ready, it.i + 1)
                    at_least(pe, cols_ready, it.i)
                    for c in range(KD):
                        tr = t.transpose(turned[:, c // 4, (c % 4) * P:(c % 4 + 1) * P],
                                         rows[:, k, c * P:(c + 1) * P], g.ident[:])
                    tr.then_inc(turned_ready, 1)
                it = item(2)
                if it:
                    k = it.buf(2)
                    pe.wait_ge(split_ready, it.i + 1)
                    at_least(pe, pre_ready, it.i - 1)
                    for c in range(KD):
                        for n, part in enumerate((hi, lo)):
                            mm = t.matmul(h1[:, k, :], part[:, k, c, :], t1[:, c, :],
                                          start=c == 0 and n == 0, stop=c == KD - 1 and n == 1)
                    mm.then_inc(h1_ready, 1)
                it = item(3)
                if it:
                    pe.wait_ge(rows2_ready, it.i + 1)
                    at_least(pe, cols2_ready, it.i)
                    for c in range(KH):
                        tr = t.transpose(turned2[:, c * P:(c + 1) * P], rows2[:, c * P:(c + 1) * P], g.ident[:])
                    tr.then_inc(turned2_ready, 1)
                it = item(4)
                if it:
                    k = it.buf(2)
                    pe.wait_ge(split2_ready, it.i + 1)
                    at_least(pe, x_ready, it.i)
                    for h in range(2):
                        for c in range(KH):
                            for n, part in enumerate((hi2, lo2)):
                                mm = t.matmul(h2[:, h, :], part[:, k, c, :], t2[:, c, h * HALF:(h + 1) * HALF],
                                              start=c == 0 and n == 0, stop=c == KH - 1 and n == 1)
                    mm.then_inc(h2_ready, 1)

            in_steps(pe, NT, 4, body, lead=2)

        @block.scalar
        def _(act):
            s = nc.scalar
            s.copy(t1[:].rearrange("p c n -> p (c n)"), g.t1[:].rearrange("p c n -> p (c n)")).then_inc(weights_ready, 1)
            act.wait_ge(small_in, 96)

            def body(item, b):
                it = item(0)
                if it:
                    k = it.buf(2)
                    act.wait_ge(mv_ready, it.i + 1)
                    s.activation(std[:, k:k + 1], mv[:, k, 1:2], ACT.Sqrt, bias=eps_eps[:, 0:1],
                                 scale=1.0 + EPS).then_inc(std_ready, 1)
                it = item(3)
                if it:
                    act.wait_ge(mv2_ready, it.i + 1)
                    s.activation(std2[:], mv2[:, 1:2], ACT.Sqrt, bias=g.eps[:, 0:1]).then_inc(std2_ready, 1)
                it = item(1)
                if it:
                    act.wait_ge(turned_ready, it.i + 1)
                    at_least(act, split_ready, it.i)
                    for c in range(KD):
                        ins = s.activation(cols[:, c, :], turned[:, c // 4, (c % 4) * P:(c % 4 + 1) * P],
                                           ACT.Identity, bias=shift1[:, c:c + 1], scale=gain1[:, c:c + 1])
                    ins.then_inc(cols_ready, 1)
                it = item(0)
                if it:
                    k = it.buf(2)
                    act.wait_ge(rstd_ready, it.i + 1)
                    at_least(act, turned_ready, it.i - 1)
                    act.sem_inc(pace, 1)
                    s.activation(rows[:, k, :], x_tile(it), ACT.Identity, bias=nmr[:, k:k + 1],
                                 scale=rstd[:, k:k + 1]).then_inc(rows_ready, 1)
                it = item(2)
                if it:
                    k = it.buf(2)
                    act.wait_ge(pre_ready, it.i + 1)
                    s.activation(hidden[:, k, :], pre[:, k, :], ACT.Gelu).then_inc(hidden_ready, 1)
                it = item(3)
                if it:
                    act.wait_ge(turned2_ready, it.i + 1)
                    at_least(act, split2_ready, it.i)
                    for c in range(KH):
                        ins = s.activation(cols2[:, c, :], turned2[:, c * P:(c + 1) * P], ACT.Identity,
                                           bias=shift2[:, c:c + 1], scale=gain2[:, c:c + 1])
                    ins.then_inc(cols2_ready, 1)

            in_steps(act, NT, 4, body, lead=2)

        @block.vector
        def _(dve):
            v = nc.vector
            st = Steps(dve, v_done)
            dve.wait_ge(small_in, 96)
            st.link(v.memset(eps_eps[:], EPS * EPS))

            def body(item, b):
                it = item(3)
                if it:
                    k = it.buf(2)
                    dve.wait_ge(hidden_ready, it.i + 1)
                    st.link(v.bn_stats(stats2[:], hidden[:, k, :]))
                    dve.sem_inc(pace, 1)
                    v.bn_aggr(mv2[:], stats2[:]).then_inc(mv2_ready, 1)
                it = item(0)
                if it:
                    k = it.buf(2)
                    at_least(dve, rows_ready, it.i - 1)
                    st.done(v.bn_stats(stats[:, k, 0, :], x_tile(it)[:, 0:HALF]))
                    st.link(v.bn_stats(stats[:, k, 1, :], x_tile(it)[:, HALF:D]))
                    dve.sem_inc(pace, 1)
                    v.bn_aggr(mv[:, k, :], stats[:, k, :, :]).then_inc(mv_ready, 1)
                it = item(3)
                if it:
                    k = it.buf(2)
                    dve.wait_ge(std2_ready, it.i + 1)
                    at_least(dve, turned2_ready, it.i)
                    st.link(v.reciprocal(rstd2[:], std2[:]))
                    v.tensor_scalar(rows2[:], hidden[:, k, :], mv2[:, 0:1], rstd2[:, 0:1], ALU.subtract,
                                    ALU.mult).then_inc(rows2_ready, 1)
                it = item(0)
                if it:
                    k = it.buf(2)
                    dve.wait_ge(std_ready, it.i + 1)
                    st.link(v.reciprocal(rstd[:, k:k + 1], std[:, k:k + 1]))
                    v.scalar_tensor_tensor(out=nmr[:, k:k + 1], in0=mv[:, k, 0:1], scalar=-1.0,
                                           in1=rstd[:, k:k + 1], op0=ALU.mult, op1=ALU.mult).then_inc(rstd_ready, 1)
                it = item(1)
                if it:
                    k = it.buf(2)
                    dve.wait_ge(cols_ready, it.i + 1)
                    at_least(dve, h1_ready, it.i - 1)
                    st.link(v.tensor_copy(hi[:, k], cols[:]))
                    v.tensor_tensor(lo[:, k], cols[:], hi[:, k].bitcast(F32), ALU.subtract).then_inc(split_ready, 1)
                it = item(2)
                if it:
                    k = it.buf(2)
                    dve.wait_ge(h1_ready, it.i + 1)
                    at_least(dve, hidden_ready, it.i - 1)
                    v.scalar_tensor_tensor(out=pre[:, k, :], in0=h1[:, k, :], scalar=g.unit[:, 0:1], in1=b1[:],
                                           op0=ALU.mult, op1=ALU.add).then_inc(pre_ready, 1)
                it = item(3)
                if it:
                    k = it.buf(2)
                    dve.wait_ge(cols2_ready, it.i + 1)
                    at_least(dve, h2_ready, it.i - 1)
                    st.link(v.tensor_copy(hi2[:, k], cols2[:]))
                    v.tensor_tensor(lo2[:, k], cols2[:], hi2[:, k].bitcast(F32), ALU.subtract).then_inc(split2_ready, 1)
                it = item(4)
                if it:
                    dve.wait_ge(h2_ready, it.i + 1)
                    dve.wait_ge(shifted, it.i + 1)
                    v.scalar_tensor_tensor(out=x_tile(it), in0=h2[:].rearrange("p h n -> p (h n)"),
                                           scalar=g.unit[:, 1:2], in1=x_tile(it), op0=ALU.mult,
                                           op1=ALU.add).then_inc(x_ready, 1)

            in_steps(dve, NT, 4, body, st, 7, lead=2)



def stage_attention_projection(nc, g):
    with ExitStack() as ctx:
        a = Alloc(nc, ctx)
        r = projection_tiles(a, "z1", False)
        r.pace = a.sem("z1_pace")
        w_hi, w_lo = a.sb("w1_hi", [P, KD, D], F32R), a.sb("w1_lo", [P, KD, D], F32R)
        raw = r.zout
        scores = a.psum("scores", [P, 2, HALF])
        raw_in = [a.sem(f"z1_raw_in{b}") for b in range(2)]
        raw_used, w_split, el_stored, v_done = (a.sem(f"z1_{n}") for n in (
            "raw_used", "w_split", "el_stored", "v_done"))
        scores_ready = a.sem("z1_scores_kept")
        x_flat = g.x_all[:].rearrange("p t d -> p (t d)")
        w_rows = g.W1.rearrange("h (c p) f -> c p h f", p=P)

        def x_of(it):
            return x_flat[:, bass.ds(it.i * D, D)]

        def x_wait(eng, it):
            pass

        block = ctx.enter_context(nc.Block())

        @block.sync
        def _(sp):
            for c in range(KD):
                if c > 1:
                    sp.wait_ge(raw_used, c - 1)
                sp.dma_start(raw[:, c % 2, :].rearrange("p (h f) -> p h f", h=HEADS), w_rows[c]).then_inc(raw_in[c % 2], 16)
            projection_sync(sp, r, None, g.z1, load=False)
            sp.wait_ge(scores_ready, NT)
            sp.dma_start(g.el.rearrange("(t p) h -> p t h", p=P), g.scores[:, :, 0:HEADS]).then_inc(el_stored, 16)
            sp.wait_ge(el_stored, 16)

        @block.scalar
        def _(act):
            for c in range(KD):
                act.wait_ge(raw_in[c % 2], 16 * (c // 2 + 1))
                nc.scalar.copy(w_hi[:, c, :], raw[:, c % 2, :]).then_inc(w_split, 1)
            projection_scalar(nc, act, r, x_of, x_wait, g.eps)

        @block.tensor
        def _(pe):
            pe.wait_ge(raw_used, KD)
            pe.wait_ge(w_split, KD)

            def extra(it):
                k = it.buf(2)
                split_products(nc.tensor, scores[:, k, 0:2 * HEADS], lambda c: (r.hi[:, k, c, :], r.lo[:, k, c, :]),
                               lambda c: (g.att_hi[:, c, :], g.att_lo[:, c, :]), KD)
            projection_tensor(nc, pe, r, w_hi, w_lo, g.ident, extra)

        @block.vector
        def _(dve):
            v = nc.vector
            st = Steps(dve, v_done)
            for c in range(KD):
                dve.wait_ge(raw_in[c % 2], 16 * (c // 2 + 1))
                dve.wait_ge(w_split, c + 1)
                v.tensor_tensor(w_lo[:, c, :], raw[:, c % 2, :], w_hi[:, c, :].bitcast(F32), ALU.subtract).then_inc(raw_used, 1)

            def extra(it):
                v.tensor_copy(g.scores[:].rearrange("p t h -> p (t h)")[:, bass.ds(it.i * 2 * HEADS, 2 * HEADS)],
                              scores[:, it.buf(2), 0:2 * HEADS]).then_inc(scores_ready, 1)
            projection_vector(nc, dve, r, st, x_of, x_wait, extra)



def stage_attention_max(nc, g):
    with ExitStack() as ctx:
        a = Alloc(nc, ctx)
        r = Named(
            rows=a.sb("m_rows", [P, 4 * GT, HEADS]), staged=a.sb("m_staged", [P, 4, GT], I32),
            gathered=[a.sem(f"m_gathered{k}") for k in range(4 * GT)],
            **{s: a.sem(f"m_{s}") for s in ("staged_ready", "multiplied", "pace")})
        away = a.sb("m_away", [P, 4, GT, P])
        masked = a.sb("m_masked", [P, 2, GT, HEADS, P])
        turned = a.psum("m_turned", [P, 2, 2, HALF])
        largest = a.sb("m_largest", [P, 2, HEADS])
        by_node = a.sb("m_by_node", [P, NT, HEADS])
        away_ready, masked_ready, turned_ready, v_done, zeroed = (
            a.sem(f"m_{n}") for n in ("away_ready", "masked_ready", "turned_ready", "v_done", "zeroed"))
        by_flat = by_node[:].rearrange("p t h -> p (t h)")
        el_flat = g.edge_el[:].rearrange("p t h -> p (t h)")

        block = ctx.enter_context(nc.Block())

        @block.gpsimd
        def _(pool):
            def body(item, b):
                it = item(0)
                if it:
                    at_least(pool, r.multiplied, it.i - 3)
                    pool.wait_ge(r.staged_ready, it.i + 1)
                    pool.sem_inc(r.pace, 1)
                    for q in range(GT):
                        slot = it.buf(4) * GT + q
                        pool.indirect_dma_start(
                            out=r.rows[:, slot, :], out_offset=None, in_=g.el,
                            in_offset=bass.IndirectOffsetOnAxis(ap=r.staged[:, it.buf(4), q:q + 1], axis=0),
                        ).then_inc(r.gathered[slot], 16)
            in_steps(pool, NG, 4, body)

        @block.scalar
        def _(act):
            s = nc.scalar

            def body(item, b):
                it = item(0)
                if it:
                    for q in range(GT):
                        at_least(act, r.gathered[it.buf(4) * GT + q], it.turn(4) * 16)
                    s.copy(r.staged[:, it.buf(4), :], g.src[:, bass.ds(it.i * GT, GT)]).then_inc(r.staged_ready, 1)
                it = item(3)
                if it:
                    k, m = it.buf(4), it.buf(2)
                    for q in range(GT):
                        act.wait_ge(r.gathered[k * GT + q], (it.turn(4) + 1) * 16)
                    act.wait_ge(away_ready, it.i + 1)
                    at_least(act, turned_ready, it.i - 1)
                    for q in range(GT):
                        for h in range(HEADS):
                            ins = s.activation(masked[:, m, q, h, :], away[:, k, q, :], ACT.Identity,
                                               bias=r.rows[:, k * GT + q, h:h + 1])
                    ins.then_inc(masked_ready, 1)
                    act.sem_inc(r.pace, 1)
                    s.copy(el_flat[:, bass.ds(it.i * GT * HEADS, GT * HEADS)],
                           r.rows[:, k * GT:(k + 1) * GT, :].rearrange("p q h -> p (q h)")).then_inc(r.multiplied, 1)
            in_steps(act, NG, 4, body)

        @block.tensor
        def _(pe):
            def body(item, b):
                it = item(0)
                if it:
                    m = it.buf(2)
                    pe.wait_ge(masked_ready, it.i + 1)
                    at_least(pe, v_done, it.i * 2 - 2)
                    for h in range(HEADS):
                        for q in range(GT):
                            tr = nc.tensor.transpose(turned[:, m, h // 2, ((h % 2) * GT + q) * P:((h % 2) * GT + q + 1) * P],
                                                     masked[:, m, q, h, :], g.ident[:])
                    tr.then_inc(turned_ready, 1)
            in_steps(pe, NG, 4, body)

        @block.vector
        def _(dve):
            v = nc.vector
            st = Steps(dve, v_done)
            v.memset(g.x_all[:].rearrange("p t d -> p (t d)"), 0.0)
            v.memset(by_node[:], -BIG)
            st.link(v.memset(g.sums[:], 0.0))

            def body(item, b):
                it = item(0)
                if it:
                    k = it.buf(4)
                    at_least(dve, masked_ready, it.i - 3)
                    for q in range(GT):
                        ins = v.tensor_scalar(away[:, k, q, :], g.iota1[:], g.place[:, bass.ds(it.i * GT + q, 1)], -BIG,
                                              ALU.not_equal, ALU.mult)
                    ins.then_inc(away_ready, 1)
                it = item(4)
                if it:
                    m = it.buf(2)
                    tile = dve.value_load(g.ntile[0:1, bass.ds(it.i, 1)], min_val=0, max_val=NT - 1)
                    to = by_flat[:, bass.ds(tile * HEADS, HEADS)]
                    dve.wait_ge(turned_ready, it.i + 1)
                    st.link(v.tensor_reduce(largest[:, m, :],
                                            turned[:, m].rearrange("p a (h n) -> p (a h) n", h=2), AX.X, ALU.max))
                    st.done(v.tensor_tensor(to, to, largest[:, m, :], ALU.max))
            in_steps(dve, NG, 4, body, st, 2)
            dve.wait_ge(v_done, st.n)
            er, shift = g.scores[:, :, HEADS:2 * HEADS], by_node[:]
            st.link(v.tensor_tensor(shift, shift, er, ALU.add))
            v.scalar_tensor_tensor(out=g.scores[:, :, 0:HEADS], in0=shift, scalar=SLOPE, in1=shift, op0=ALU.mult,
                                   op1=ALU.max)



def stage_second_graph(nc, g):
    with ExitStack() as ctx:
        a = Alloc(nc, ctx)
        r = Named(
            rows=a.sb("g1_rows", [P, 4 * GT, D]), staged=a.sb("g1_staged", [P, 4, GT], I32),
            gathered=[a.sem(f"g1_gathered{k}") for k in range(4 * GT)],
            **{s: a.sem(f"g1_{s}") for s in ("staged_ready", "multiplied", "pace")})
        goes = a.sb("g1_goes", [P, 4, GT, P], F32R)
        comes = a.sb("g1_comes", [P, 2, GT, P], F32R)
        ident = a.sb("g1_ident", [P, P], F32R)
        parts = a.sb("g1_parts", [P, NT, 2, 2 * HEADS], F32R)
        node = a.sb("g1_node", [P, 4, 2, 2 * HEADS], F32R)
        factor = a.sb("g1_factor", [P, 4, GT, HEADS])
        score = a.sb("g1_score", [P, GT, HEADS])
        share = a.sb("g1_share", [P, 2, HEADS, P])
        scaled_hi, scaled_lo = a.sb("g1_scaled_hi", [P, 2, D], F32R), a.sb("g1_scaled_lo", [P, 2, D], F32R)
        turned = a.psum("g1_turned", [P, HALF])
        of_edge_bank = a.psum("g1_of_edge", [P, HALF])
        of_edge = of_edge_bank[:, 0:GT * 2 * HEADS].rearrange("p (q h) -> p q h", q=GT)
        sums, totals = a.psum("g1_sums", [P, 2, 2, HALF]), a.psum("g1_totals", [P, 2, HALF])
        (parts_ready, goes_ready, turned_ready, comes_ready, node_ready, of_edge_ready, score_ready, factor_ready,
         share_v, share_a, scaled_ready, split_ready, added, v_done) = (
            a.sem(f"g1_{n}") for n in (
                "parts_ready", "goes_ready", "turned_ready", "comes_ready", "node_ready", "of_edge_ready",
                "score_ready", "factor_ready", "share_v", "share_a", "scaled_ready",
                "split_ready", "added", "v_done"))
        flat = g.x_all[:].rearrange("p t d -> p (t d)")
        totals_flat = g.sums[:].rearrange("p t h -> p (t h)")
        parts_flat = parts[:].rearrange("p t a h -> p (t a h)")

        block = ctx.enter_context(nc.Block())

        @block.gpsimd
        def _(pool):
            gather_groups(nc, pool, r, g, g.z1)

        @block.scalar
        def _(act):
            s = nc.scalar
            act.wait_ge(parts_ready, 1)

            def body(item, b):
                it = item(1)
                if it:
                    m = it.buf(2)
                    act.wait_ge(turned_ready, it.i + 1)
                    at_least(act, of_edge_ready, it.i - 1)
                    s.copy(comes[:, m].rearrange("p q n -> p (q n)"),
                           turned[:, 0:GT * P]).then_inc(comes_ready, 1)
                it = item(0)
                if it:
                    k = it.buf(4)
                    at_least(act, of_edge_ready, it.i - 3)
                    act.sem_inc(r.pace, 1)
                    tile = act.value_load(g.ntile[0:1, bass.ds(it.i, 1)], min_val=0, max_val=NT - 1)
                    s.copy(node[:, k].rearrange("p a h -> p (a h)"),
                           parts_flat[:, bass.ds(tile * 4 * HEADS, 4 * HEADS)]).then_inc(node_ready, 1)
                it = item(2)
                if it:
                    k, m = it.buf(4), it.buf(2)
                    act.wait_ge(r.gathered[k * GT + 1], (it.turn(4) + 1) * 16)
                    act.wait_ge(factor_ready, it.i + 1)
                    at_least(act, r.multiplied, it.i - 1)
                    for h in range(HEADS):
                        cols = slice(h * HF, (h + 1) * HF)
                        ins = s.activation(scaled_hi[:, m, cols], r.rows[:, k * GT + 1, cols], ACT.Copy,
                                           scale=factor[:, k, 1, h:h + 1])
                    ins.then_inc(scaled_ready, 1)
                    for h in range(2, HEADS):
                        ins = s.activation(share[:, m, h, :], goes[:, k, 0, :].bitcast(F32), ACT.Copy,
                                           scale=factor[:, k, 0, h:h + 1])
                    ins.then_inc(share_a, 1)
                it = item(1)
                if it:
                    k = it.buf(4)
                    act.wait_ge(score_ready, it.i + 1)
                    at_least(act, r.multiplied, it.i - 3)
                    s.activation(factor[:, k].rearrange("p q h -> p (q h)"), score[:].rearrange("p q h -> p (q h)"),
                                 ACT.Exp).then_inc(factor_ready, 1)
            in_steps(act, NG, 4, body, lead=2)

        @block.tensor
        def _(pe):
            t = nc.tensor
            pe.wait_ge(parts_ready, 1)

            def body(item, b):
                it = item(3)
                if it:
                    k, m = it.buf(4), it.buf(2)
                    pe.wait_ge(scaled_ready, it.i + 1)
                    at_least(pe, added, it.i - 1)
                    for c in range(2):
                        t.matmul(sums[:, m, c, :], goes[:, k, 1, :], scaled_hi[:, m, c * HALF:(c + 1) * HALF],
                                 start=True, stop=False)
                it = item(1)
                if it:
                    m = it.buf(2)
                    pe.wait_ge(comes_ready, it.i + 1)
                    pe.wait_ge(node_ready, it.i + 1)
                    at_least(pe, score_ready, it.i)
                    for q in range(GT):
                        for n in range(2):
                            mm = t.matmul(of_edge[:, q, :], comes[:, m, q, :], node[:, it.buf(4), n, :],
                                          start=n == 0, stop=n == 1)
                    mm.then_inc(of_edge_ready, 1)
                it = item(3)
                if it:
                    k, m = it.buf(4), it.buf(2)
                    pe.wait_ge(share_v, it.i + 1)
                    pe.wait_ge(share_a, it.i + 1)
                    pe.wait_ge(r.gathered[k * GT], (it.turn(4) + 1) * 16)
                    for h in range(HEADS):
                        t.matmul(sums[:, m, h // 2, h % 2 * HF:(h % 2 + 1) * HF], share[:, m, h, :],
                                 r.rows[:, k * GT, h * HF:(h + 1) * HF], start=False, stop=False)
                    pe.wait_ge(split_ready, it.i + 1)
                    for c in range(2):
                        t.matmul(sums[:, m, c, :], goes[:, k, 1, :], scaled_lo[:, m, c * HALF:(c + 1) * HALF],
                                 start=False, stop=True)
                    for q in range(GT):
                        mm = t.matmul(totals[:, m, 0:HEADS], goes[:, k, q, :].bitcast(F32), factor[:, k, q, :],
                                      start=q == 0, stop=q == GT - 1)
                    mm.then_inc(r.multiplied, 1)
                it = item(0)
                if it:
                    pe.wait_ge(goes_ready, it.i + 1)
                    at_least(pe, comes_ready, it.i)
                    for q in range(GT):
                        tr = t.matmul(turned[:, q * P:(q + 1) * P], goes[:, it.buf(4), q, :], ident[:],
                                      start=True, stop=True)
                    tr.then_inc(turned_ready, 1)
            in_steps(pe, NG, 4, body, lead=2)

        @block.vector
        def _(dve):
            v = nc.vector
            st = Steps(dve, v_done)
            v.tensor_copy(ident[:], g.ident[:])
            st.link(v.tensor_copy(parts[:, :, 0, :], g.scores[:]))
            v.tensor_tensor(parts[:, :, 1, :], g.scores[:], parts[:, :, 0, :].bitcast(F32),
                            ALU.subtract).then_inc(parts_ready, 1)

            def body(item, b):
                it = item(4)
                if it:
                    m = it.buf(2)
                    tile = dve.value_load(g.ntile[0:1, bass.ds(it.i, 1)], min_val=0, max_val=NT - 1)
                    to, tot = flat[:, bass.ds(tile * D, D)], totals_flat[:, bass.ds(tile * HEADS, HEADS)]
                    dve.wait_ge(r.multiplied, it.i + 1)
                    at_least(dve, added, it.i)
                    v.tensor_tensor(tot, tot, totals[:, m, 0:HEADS], ALU.add)
                    v.tensor_tensor(to, to, sums[:, m].rearrange("p h n -> p (h n)"), ALU.add).then_inc(added, 1)
                new, it = item(0), item(1)
                flat_score = score[:].rearrange("p q h -> p (q h)")
                if it:
                    dve.wait_ge(of_edge_ready, it.i + 1)
                    at_least(dve, factor_ready, it.i)
                    st.done(v.tensor_tensor(score[:], g.edge_el[:, bass.ds(it.i * GT, GT), :],
                                            of_edge[:, :, HEADS:2 * HEADS], ALU.add))
                if new:
                    at_least(dve, r.multiplied, new.i - 3)
                    dve.sem_inc(r.pace, 1)
                    v.tensor_scalar(goes[:, new.buf(4), 0, :], g.iota1[:], g.place[:, bass.ds(new.i * GT, 1)], None,
                                    ALU.is_equal)
                if it:
                    dve.wait_ge(v_done, st.n)
                    st.done(v.scalar_tensor_tensor(out=flat_score, in0=flat_score, scalar=SLOPE, in1=flat_score,
                                                   op0=ALU.mult, op1=ALU.max))
                if new:
                    v.tensor_scalar(goes[:, new.buf(4), 1, :], g.iota1[:], g.place[:, bass.ds(new.i * GT + 1, 1)], None,
                                    ALU.is_equal).then_inc(goes_ready, 1)
                if it:
                    dve.wait_ge(v_done, st.n)
                    st.link(v.tensor_tensor(score[:], score[:], of_edge[:, :, 0:HEADS], ALU.subtract))
                    v.tensor_scalar(flat_score, flat_score, 0.0, None, ALU.min).then_inc(score_ready, 1)
                it = item(2)
                if it:
                    k, m = it.buf(4), it.buf(2)
                    dve.wait_ge(factor_ready, it.i + 1)
                    at_least(dve, r.multiplied, it.i - 1)
                    for h in range(2):
                        ins = v.tensor_scalar(share[:, m, h, :], goes[:, k, 0, :].bitcast(F32), factor[:, k, 0, h:h + 1],
                                              None, ALU.mult)
                    ins.then_inc(share_v, 1)
                    dve.wait_ge(scaled_ready, it.i + 1)
                    for h in range(HEADS):
                        cols = slice(h * HF, (h + 1) * HF)
                        ins = v.scalar_tensor_tensor(out=scaled_lo[:, m, cols], in0=r.rows[:, k * GT + 1, cols],
                                                     scalar=factor[:, k, 1, h:h + 1],
                                                     in1=scaled_hi[:, m, cols].bitcast(F32), op0=ALU.mult,
                                                     op1=ALU.subtract)
                    ins.then_inc(split_ready, 1)
            in_steps(dve, NG, 4, body, st, 3, lead=2)



def split_vector(v, low, whole, high, ready):
    v.tensor_tensor(low, whole, high.bitcast(F32), ALU.subtract).then_inc(ready, 1)


def expert_hidden(t, out, w_hi, w_lo, x_hi, x_lo):
    for m in range(EH // P):
        cols = slice(m * P, (m + 1) * P)
        mm = split_products(t, out[:, m * GT * P:(m + 1) * GT * P], lambda c: (w_hi[:, c, cols], w_lo[:, c, cols]),
                            lambda c: (x_hi[:, c, :], x_lo[:, c, :]), KD)
    return mm


def expert_output(t, out, h_hi, h_lo, w_hi, w_lo, q):
    tokens = slice(q * P, (q + 1) * P)
    for h in range(2):
        cols = slice(h * HALF, (h + 1) * HALF)
        mm = split_products(t, out[:, h, :], lambda m: (h_hi[:, m, tokens], h_lo[:, m, tokens]),
                            lambda m: (w_hi[:, m, cols], w_lo[:, m, cols]), EH // P)
    return mm



def stage_shared_expert(nc, g):
    with ExitStack() as ctx:
        a = Alloc(nc, ctx)
        sb = lambda n, s, dt=F32: a.sb(f"s_{n}", s, dt)
        w1_hi, w1_lo = sb("w1_hi", [P, KD, EH], F32R), sb("w1_lo", [P, KD, EH], F32R)
        w2_hi, w2_lo = sb("w2_hi", [P, 2, D], F32R), sb("w2_lo", [P, 2, D], F32R)
        rw_hi, rw_lo = sb("rw_hi", [P, KD, EXPERTS], F32R), sb("rw_lo", [P, KD, EXPERTS], F32R)
        rw, bias1, bias2 = sb("rw", [P, KD, EXPERTS]), sb("bias1", [P, 2]), sb("bias2", [P, D])
        router_b = sb("router_b", [P, EXPERTS])
        x2 = sb("x2", [P, 2, GT, D])
        rows = sb("rows", [P, 2, GT, D])
        raw = rows[:].rearrange("p a q d -> p a (q d)")
        hi, lo = sb("hi", [P, KD, GT * P], F32R), sb("lo", [P, KD, GT * P], F32R)
        act_out = sb("act_out", [P, 2 * GT * P])
        h_hi, h_lo = sb("h_hi", [P, 2, GT * P], F32R), sb("h_lo", [P, 2, GT * P], F32R)
        inverse = sb("inverse", [P, NT * HEADS])
        stats, mv = sb("stats", [P, 2, GT, 2, 6]), sb("mv", [P, 2, GT, 2])
        std, rstd, nmr = (sb(n, [P, 2, GT]) for n in ("std", "rstd", "nmr"))
        turned, y = a.psum("s_turned", [P, 2, HALF]), a.psum("s_y", [P, GT, 2, HALF])
        hidden, logit = a.psum("s_hidden", [P, HALF]), a.psum("s_logit", [P, HALF])
        flat = g.x_all[:].rearrange("p t d -> p (t d)")
        logits_flat = g.logits[:].rearrange("p t e -> p (t e)")

        names = ("small_in raw_in w_high w_low v_done mv_ready std_ready rstd_ready rows_ready turned_ready hi_ready "
                 "lo_ready hidden_ready act_ready split_ready y_ready y_added logit_ready logit_kept x3_ready "
                 "shifted pace").split()
        m = Named(**{n: a.sem(f"s_{n}") for n in names})
        x2_in = [a.sem(f"s_x2_in{k}") for k in range(2)]
        rows_out, x_out = [a.sem(f"s_rows_out{k}") for k in range(2)], a.sem("s_x_out")
        raw_in = [a.sem(f"s_raw_in{k}") for k in range(2)]

        def x_tile(it, q):
            return flat[:, bass.ds((it.i * GT + q) * D, D)]

        block = ctx.enter_context(nc.Block())

        @block.sync
        def _(sp):
            sp.dma_start(raw[:, 0, :].rearrange("p (c f) -> p c f", c=KD),
                         g.sw1.rearrange("(c p) f -> p c f", p=P)).then_inc(raw_in[0], 16)
            sp.dma_start(raw[:, 1, :].rearrange("p (m n) -> p m n", m=2),
                         g.sw2.rearrange("(m p) n -> p m n", p=P)).then_inc(raw_in[1], 16)
            sp.dma_start(rw[:], g.router_w.rearrange("(c p) e -> p c e", p=P)).then_inc(m.small_in, 16)
            with nc.allow_non_contiguous_dma(reason="a few hundred parameters"):
                sp.dma_start(bias1[:], g.sb1.rearrange("(m p) -> p m", p=P)).then_inc(m.small_in, 16)
            sp.dma_start(bias2[:], g.sb2.partition_broadcast(P)).then_inc(m.small_in, 16)
            sp.dma_start(router_b[:], g.router_b.partition_broadcast(P)).then_inc(m.small_in, 16)

            def body(item, b):
                it = item(0)
                if it:
                    k = it.buf(2)
                    at_least(sp, m.x3_ready, (it.i - 1) * GT)
                    sp.dma_start(x2[:, k], g.x2[bass.ds(it.i * GT * P, GT * P), :].rearrange(
                        "(q p) d -> p q d", p=P)).then_inc(x2_in[k], 16)
                    sp.wait_ge(m.rows_ready, (it.i + 1) * GT)
                    sp.dma_start(g.xn3[bass.ds(it.i * GT * P, GT * P), :].rearrange("(q p) d -> p q d", p=P),
                                 rows[:, k]).then_inc(rows_out[k], 16)
                it = item(2)
                if it:
                    sp.wait_ge(m.y_added, (it.i + 1) * GT)
                    sp.dma_start(g.x4[bass.ds(it.i * GT * P, GT * P), :].rearrange("(q p) d -> p q d", p=P),
                                 flat[:, bass.ds(it.i * GT * D, GT * D)].rearrange("p (q d) -> p q d", q=GT)).then_inc(x_out, 16)
            in_steps(sp, NT // GT, 2, body, lead=2)
            for k in range(2):
                sp.wait_ge(rows_out[k], 16 * (NT // GT // 2))
            sp.wait_ge(x_out, 16 * (NT // GT))

        @block.gpsimd
        def _(pool):
            pool.wait_ge(m.small_in, 64)

            def body(item, b):
                it = item(1)
                if it:
                    for q in range(GT):
                        pool.wait_ge(m.rows_ready, it.i * GT + q + 1)
                        pool.sem_inc(m.pace, 1)
                        nc.gpsimd.tensor_tensor(x_tile(it, q), x_tile(it, q), bias2[:], ALU.add).then_inc(m.shifted, 1)
            in_steps(pool, NT // GT, 2, body, lead=2)

        @block.tensor
        def _(pe):
            t = nc.tensor
            pe.wait_ge(m.w_low, 3)

            def body(item, b):
                for q in range(GT):
                    it = item(1)
                    if it:
                        n = it.i * GT + q
                        pe.wait_ge(m.rows_ready, n + 1)
                        at_least(pe, m.lo_ready, n)
                        for c in range(KD):
                            tr = t.transpose(turned[:, c // 4, (c % 4) * P:(c % 4 + 1) * P],
                                             rows[:, it.buf(2), q, c * P:(c + 1) * P], g.ident[:])
                        tr.then_inc(m.turned_ready, 1)
                    it = item(2)
                    if it:
                        n = it.i * GT + q
                        pe.wait_ge(m.split_ready, it.i + 1)
                        at_least(pe, m.y_added, n - 1)
                        expert_output(t, y[:, q], h_hi, h_lo, w2_hi, w2_lo, q).then_inc(m.y_ready, 1)
                it = item(1)
                if it:
                    pe.wait_ge(m.lo_ready, (it.i + 1) * GT)
                    pe.wait_ge(m.hi_ready, (it.i + 1) * GT)
                    at_least(pe, m.act_ready, it.i)
                    expert_hidden(t, hidden, w1_hi, w1_lo, hi, lo).then_inc(m.hidden_ready, 1)
                    at_least(pe, m.logit_kept, it.i)
                    for q in range(GT):
                        tokens = slice(q * P, (q + 1) * P)
                        mm = split_products(t, logit[:, q * EXPERTS:(q + 1) * EXPERTS],
                                            lambda c: (hi[:, c, tokens], lo[:, c, tokens]),
                                            lambda c: (rw_hi[:, c, :], rw_lo[:, c, :]), KD)
                    mm.then_inc(m.logit_ready, 1)
            in_steps(pe, NT // GT, 2, body, lead=2)

        @block.scalar
        def _(act):
            s = nc.scalar
            for k, high in enumerate((w1_hi, w2_hi)):
                act.wait_ge(raw_in[k], 16)
                s.copy(high[:].rearrange("p a b -> p (a b)"), raw[:, k, :]).then_inc(m.w_high, 1)
            act.wait_ge(m.small_in, 64)
            s.copy(rw_hi[:], rw[:]).then_inc(m.w_high, 1)
            act.wait_ge(m.w_low, 2)

            def high(it, q):
                n = it.i * GT + q
                act.wait_ge(m.turned_ready, n + 1)
                at_least(act, m.logit_ready, it.i)
                s.copy(hi[:, :, q * P:(q + 1) * P], turned[:].rearrange("p h (c n) -> p (h c) n", n=P)).then_inc(m.hi_ready, 1)

            def body(item, b):
                for q in range(GT):
                    if item(1):
                        high(item(1), q)
                    it = item(0)
                    if it:
                        k = it.buf(2)
                        act.wait_ge(m.mv_ready, it.i * GT + q + 1)
                        s.activation(std[:, k, q:q + 1], mv[:, k, q, 1:2], ACT.Sqrt, bias=g.eps[:, 0:1]).then_inc(m.std_ready, 1)
                it = item(0)
                if it:
                    k = it.buf(2)
                    at_least(act, rows_out[k], it.turn(2) * 16)
                    for q in range(GT):
                        act.wait_ge(m.rstd_ready, it.i * GT + q + 1)
                        act.sem_inc(m.pace, 1)
                        s.activation(rows[:, k, q, :], x_tile(it, q), ACT.Identity, bias=nmr[:, k, q:q + 1],
                                     scale=rstd[:, k, q:q + 1]).then_inc(m.rows_ready, 1)
                it = item(1)
                if it:
                    act.wait_ge(m.hidden_ready, it.i + 1)
                    at_least(act, m.split_ready, it.i)
                    for c in range(2):
                        cols = slice(c * GT * P, (c + 1) * GT * P)
                        ins = s.activation(act_out[:, cols], hidden[:, cols], ACT.Gelu, bias=bias1[:, c:c + 1])
                    ins.then_inc(m.act_ready, 1)
            in_steps(act, NT // GT, 2, body, lead=2)

        @block.vector
        def _(dve):
            v = nc.vector
            st = Steps(dve, m.v_done)
            for k, (low, high) in enumerate(((w1_lo, w1_hi), (w2_lo, w2_hi))):
                dve.wait_ge(m.w_high, k + 1)
                dve.wait_ge(raw_in[k], 16)
                split_vector(v, low[:].rearrange("p a b -> p (a b)"), raw[:, k, :],
                             high[:].rearrange("p a b -> p (a b)"), m.w_low)
            dve.wait_ge(m.w_high, 3)
            dve.wait_ge(m.small_in, 64)
            split_vector(v, rw_lo[:], rw[:], rw_hi[:], m.w_low)
            st.link(v.tensor_scalar(inverse[:], g.sums[:].rearrange("p t h -> p (t h)"), 1e-20, None, ALU.max))
            st.link(v.reciprocal(inverse[:], inverse[:]))

            def low(it, q):
                dve.wait_ge(m.hi_ready, it.i * GT + q + 1)
                tokens = slice(q * P, (q + 1) * P)
                v.tensor_tensor(lo[:, :, tokens], turned[:].rearrange("p h (c n) -> p (h c) n", n=P),
                                hi[:, :, tokens].bitcast(F32), ALU.subtract).then_inc(m.lo_ready, 1)

            def body(item, b):
                for q in range(GT):
                    if item(1):
                        low(item(1), q)
                    it = item(0)
                    if it:
                        k = it.buf(2)
                        x = x_tile(it, q)
                        if q == 0:
                            dve.wait_ge(x2_in[k], (it.turn(2) + 1) * 16)
                            at_least(dve, m.rows_ready, (it.i - 1) * GT)
                        for h in range(HEADS):
                            cols = slice(h * HF, (h + 1) * HF)
                            x_h = flat[:, bass.ds((it.i * GT + q) * D + h * HF, HF)]
                            ins = v.scalar_tensor_tensor(out=x_h, in0=x_h,
                                                         scalar=inverse[:, bass.ds((it.i * GT + q) * HEADS + h, 1)],
                                                         in1=x2[:, k, q, cols], op0=ALU.mult, op1=ALU.add)
                        ins.then_inc(m.x3_ready, 1)
                        dve.wait_ge(m.x3_ready, it.i * GT + q + 1)
                        dve.sem_inc(m.pace, 1)
                        st.done(v.bn_stats(stats[:, k, q, 0, :], x[:, 0:HALF]))
                        st.link(v.bn_stats(stats[:, k, q, 1, :], x[:, HALF:D]))
                        dve.sem_inc(m.pace, 1)
                        v.bn_aggr(mv[:, k, q, :], stats[:, k, q]).then_inc(m.mv_ready, 1)
                    it = item(2)
                    if it:
                        n = it.i * GT + q
                        dve.wait_ge(m.y_ready, n + 1)
                        dve.wait_ge(m.shifted, n + 1)
                        v.tensor_tensor(x_tile(it, q), x_tile(it, q), y[:, q].rearrange("p h n -> p (h n)"),
                                        ALU.add).then_inc(m.y_added, 1)
                it = item(0)
                if it:
                    k = it.buf(2)
                    for q in range(GT):
                        dve.wait_ge(m.std_ready, it.i * GT + q + 1)
                        st.link(v.reciprocal(rstd[:, k, q:q + 1], std[:, k, q:q + 1]))
                        v.scalar_tensor_tensor(out=nmr[:, k, q:q + 1], in0=mv[:, k, q, 0:1], scalar=-1.0,
                                               in1=rstd[:, k, q:q + 1], op0=ALU.mult, op1=ALU.mult).then_inc(m.rstd_ready, 1)
                it = item(1)
                if it:
                    dve.wait_ge(m.act_ready, it.i + 1)
                    at_least(dve, m.y_ready, it.i * GT)
                    whole = act_out[:].rearrange("p (m n) -> p m n", m=2)
                    st.link(v.tensor_copy(h_hi[:], whole))
                    split_vector(v, h_lo[:], whole, h_hi[:], m.split_ready)
                    dve.wait_ge(m.logit_ready, it.i + 1)
                    for q in range(GT):
                        ins = v.tensor_tensor(logits_flat[:, bass.ds((it.i * GT + q) * EXPERTS, EXPERTS)],
                                              logit[:, q * EXPERTS:(q + 1) * EXPERTS], router_b[:], ALU.add)
                    ins.then_inc(m.logit_kept, 1)
            in_steps(dve, NT // GT, 2, body, st, 2 * GT + GT + 1, lead=2)



def stage_route(nc, g):
    with ExitStack() as ctx:
        a = Alloc(nc, ctx)
        sb = lambda n, s, dt=F32: a.sb(f"r_{n}", s, dt)
        o = sort_tiles(a, "psort", NPAIR, EXPERTS, PG)
        iota_e, later_e = sb("iota_e", [P, NT, EXPERTS]), sb("later_e", [P, NT, EXPERTS])
        token, valid = sb("token", [P, TOPK, NT]), sb("valid", [P, TOPK, NT])
        iota_r, iota_c = sb("iota_r", [P, P]), sb("iota_c", [P, PT])
        probs, left, hit = (sb(n, [P, NT, EXPERTS]) for n in ("probs", "left", "hit"))
        top = sb("top", [P, NT])
        expert = sb("expert", [P, TOPK, NT])
        place_i, col_i, row_i = (sb(n, [P, NPAIR], I32) for n in ("place_i", "col_i", "row_i"))
        col, row = sb("col", [P, NPAIR]), sb("row", [P, NPAIR])
        at_row, at_col = sb("at_row", [P, 2, P], F32R), sb("at_col", [P, 2, PT], F32R)
        sorted_tokens = a.psum("r_sorted_tokens", [P, HALF])
        ready, v_done, shifted, exps, pair_ready, pair_used = (
            a.sem(f"r_{n}") for n in ("ready", "v_done", "shifted", "exps", "pair_ready", "pair_used"))

        block = ctx.enter_context(nc.Block())

        @block.gpsimd
        def _(pool):
            q = nc.gpsimd
            small = dict(allow_small_or_imprecise_dtypes=True)
            q.iota(iota_e[:], pattern=[[0, NT], [1, EXPERTS]], base=0, channel_multiplier=0, **small)
            q.iota(token[:], pattern=[[0, TOPK], [P, NT]], base=0, channel_multiplier=1, **small)
            q.iota(iota_r[:], pattern=[[1, P]], base=0, channel_multiplier=0, **small)
            q.iota(iota_c[:], pattern=[[1, PT]], base=0, channel_multiplier=0, **small)
            sort_constants(nc, pool, o, NPAIR, EXPERTS, PG, ready, 0)

        @block.scalar
        def _(act):
            act.wait_ge(shifted, 1)
            nc.scalar.activation(probs[:], probs[:], ACT.Exp).then_inc(exps, 1)

        @block.tensor
        def _(pe):
            pe.wait_ge(ready, 2)
            sort_tensor(nc, pe, o, slice(0, P), NPAIR, EXPERTS)

            def pair(c, k, start=False, stop=False):
                pe.wait_ge(pair_ready, c + 1)
                nc.tensor.matmul(sorted_tokens[:, 0:PT], at_row[:, k, :], at_col[:, k, :], start=start,
                                 stop=stop).then_inc(pair_used, 1)
            pair(0, 0, start=True)
            pair(1, 1)
            with pe.Fori(1, NPAIR // 2 - 1) as j:
                for k in range(2):
                    pair(j * 2 + k, k)
            pair(NPAIR - 2, 0)
            pair(NPAIR - 1, 1, stop=True)

        @block.vector
        def _(dve):
            v = nc.vector
            st = Steps(dve, v_done)
            wide = lambda t: t.unsqueeze(2).to_broadcast([P, NT, EXPERTS])
            dve.wait_ge(ready, 2)
            st.link(v.tensor_reduce(top[:], g.logits[:], AX.X, ALU.max))
            v.tensor_tensor(probs[:], g.logits[:], wide(top[:]), ALU.subtract).then_inc(shifted, 1)
            dve.wait_ge(exps, 1)
            st.link(v.tensor_reduce(top[:], probs[:], AX.X, ALU.add))
            st.link(v.reciprocal(top[:], top[:]))
            st.link(v.tensor_tensor(probs[:], probs[:], wide(top[:]), ALU.mult))
            st.done(v.tensor_copy(left[:], probs[:]))
            st.link(v.tensor_scalar(later_e[:], iota_e[:], -1.0, float(EXPERTS), ALU.mult, ALU.add))
            for k in range(TOPK):
                st.link(v.tensor_reduce(g.top_prob[:, k, :], left[:], AX.X, ALU.max))
                st.link(v.tensor_tensor(hit[:], left[:], wide(g.top_prob[:, k, :]), ALU.is_equal))
                st.link(v.tensor_tensor(hit[:], hit[:], later_e[:], ALU.mult))
                st.link(v.tensor_reduce(top[:], hit[:], AX.X, ALU.max))
                st.link(v.tensor_scalar(expert[:, k, :], top[:], -1.0, float(EXPERTS), ALU.mult, ALU.add))
                if k + 1 < TOPK:
                    st.link(v.tensor_tensor(hit[:], iota_e[:], wide(expert[:, k, :]), ALU.is_equal))
                    st.link(v.scalar_tensor_tensor(out=left[:], in0=hit[:], scalar=-2.0, in1=left[:], op0=ALU.mult,
                                                   op1=ALU.add))
            st.link(v.tensor_scalar(valid[:], token[:], float(N_NODES), None, ALU.is_lt))
            bucket = o.bucket[:].rearrange("p (k t) -> p k t", k=TOPK)
            st.link(v.tensor_scalar(bucket, expert[:], -float(EXPERTS), None, ALU.add))
            st.link(v.tensor_tensor(bucket, bucket, valid[:], ALU.mult))
            st.link(v.tensor_scalar(bucket, bucket, float(EXPERTS), None, ALU.add))
            sort_vector(nc, dve, st, o, slice(0, P), NPAIR, EXPERTS)
            st.done(v.tensor_scalar(g.expert[:], o.of_group[:], float(EXPERTS - 1), None, ALU.min))
            place = o.place[:].rearrange("p (k t) -> p k t", k=TOPK)
            st.link(v.tensor_scalar(valid[:], valid[:], -float(PT * P), float(PT * P), ALU.mult, ALU.add))
            st.link(v.tensor_tensor(place, place, valid[:], ALU.add))
            st.link(v.tensor_copy(place_i[:], o.place[:]))
            st.done(v.tensor_scalar(g.pair_place[:], place_i[:], float(PT * P - 1), None, ALU.min))
            st.done(v.tensor_scalar(col_i[:], place_i[:], 7, None, ALU.arith_shift_right))
            st.link(v.tensor_scalar(row_i[:], place_i[:], P - 1, None, ALU.bitwise_and))
            st.done(v.tensor_copy(col[:], col_i[:]))
            st.link(v.tensor_copy(row[:], row_i[:]))
            tokens = token[:].rearrange("p k t -> p (k t)")

            def pair(c, k):
                at_least(dve, pair_used, c - 1)
                v.tensor_scalar(at_row[:, k, :], iota_r[:], row[:, bass.ds(c, 1)], tokens[:, bass.ds(c, 1)],
                                ALU.is_equal, ALU.mult)
                v.tensor_scalar(at_col[:, k, :], iota_c[:], col[:, bass.ds(c, 1)], None,
                                ALU.is_equal).then_inc(pair_ready, 1)
            pair(0, 0)
            pair(1, 1)
            with dve.Fori(1, NPAIR // 2) as j:
                for k in range(2):
                    pair(j * 2 + k, k)
            dve.wait_ge(pair_used, NPAIR)
            v.tensor_copy(g.sorted_token[:], sorted_tokens[:, 0:PT])



def stage_experts(nc, g):
    with ExitStack() as ctx:
        a = Alloc(nc, ctx)
        sb = lambda n, s, dt=F32: a.sb(f"e_{n}", s, dt)
        raw1, raw2 = sb("raw1", [P, KD * EH]), sb("raw2", [P, 2 * D])
        w1_hi, w1_lo = sb("w1_hi", [P, 2, KD, EH], F32R), sb("w1_lo", [P, 2, KD, EH], F32R)
        w2_hi, w2_lo = sb("w2_hi", [P, 2, 2, D], F32R), sb("w2_lo", [P, 2, 2, D], F32R)
        all_bias1, bias1, bias2 = sb("all_bias1", [P, EXPERTS * 2]), sb("bias1", [P, 2, 2]), sb("bias2", [P, 2, D])
        rows, staged = sb("rows", [P, 2, GT, D]), sb("staged", [P, 2, GT], I32)
        hi, lo = sb("hi", [P, KD, GT * P], F32R), sb("lo", [P, KD, GT * P], F32R)
        act_out = sb("act_out", [P, 2 * GT * P])
        h_hi, h_lo = sb("h_hi", [P, 2, GT * P], F32R), sb("h_lo", [P, 2, GT * P], F32R)
        y_out = sb("y_out", [P, 2, GT, D])
        turned, y = a.psum("e_turned", [P, 2, HALF]), a.psum("e_y", [P, GT, 2, HALF])
        hidden = a.psum("e_hidden", [P, HALF])
        names = ("small_in raw1_in raw2_in raw1_used raw2_used w1_high w2_high v_done staged_ready turned_ready "
                 "hi_ready lo_ready hidden_ready act_ready split_ready y_ready y_kept bias1_ready pace").split()
        m = Named(**{n: a.sem(f"e_{n}") for n in names})
        gathered = [[a.sem(f"e_gathered{k}{q}") for q in range(GT)] for k in range(2)]
        bias2_in, y_stored = [a.sem(f"e_bias2_in{k}") for k in range(2)], [a.sem(f"e_y_stored{k}") for k in range(2)]

        block = ctx.enter_context(nc.Block())

        @block.sync
        def _(sp):
            with nc.allow_non_contiguous_dma(reason="two thousand parameters"):
                for c in range(2):
                    sp.dma_start(all_bias1[:].rearrange("p (e m) -> p m e", m=2)[:, c, :],
                                 g.rb1.rearrange("e (m p) -> m p e", p=P)[c]).then_inc(m.small_in, 16)

            def body(item, b):
                it = item(0)
                if it:
                    k = it.buf(2)
                    e = sp.value_load(g.expert[0:1, bass.ds(it.i, 1)], min_val=0, max_val=EXPERTS - 1)
                    at_least(sp, m.raw1_used, it.i)
                    sp.dma_start(raw1[:].rearrange("p (c f) -> p c f", c=KD),
                                 g.rw1.rearrange("e (c p) f -> p (e c) f", p=P)[:, bass.ds(e * KD, KD), :]).then_inc(m.raw1_in, 16)
                    at_least(sp, m.raw2_used, it.i)
                    sp.dma_start(raw2[:].rearrange("p (m n) -> p m n", m=2),
                                 g.rw2.rearrange("e (m p) n -> p (e m) n", p=P)[:, bass.ds(e * 2, 2), :]).then_inc(m.raw2_in, 16)
                    at_least(sp, m.y_kept, (it.i - 1) * GT)
                    sp.dma_start(bias2[:, k, :], g.rb2.rearrange("e d -> (e d)")[bass.ds(e * D, D)].partition_broadcast(P)).then_inc(bias2_in[k], 16)
                it = item(2)
                if it:
                    k = it.buf(2)
                    sp.wait_ge(m.y_kept, (it.i + 1) * GT)
                    sp.dma_start(g.y[bass.ds(it.i * GT * P, GT * P), :].rearrange("(q p) d -> p q d", p=P),
                                 y_out[:, k]).then_inc(y_stored[k], 16)
            in_steps(sp, PG, 2, body, lead=2)
            for k in range(2):
                sp.wait_ge(y_stored[k], 16 * (PG // 2))

        @block.gpsimd
        def _(pool):
            def body(item, b):
                it = item(0)
                if it:
                    k = it.buf(2)
                    at_least(pool, m.turned_ready, (it.i - 1) * GT)
                    pool.wait_ge(m.staged_ready, it.i + 1)
                    pool.sem_inc(m.pace, 1)
                    for q in range(GT):
                        pool.indirect_dma_start(
                            out=rows[:, k, q, :], out_offset=None, in_=g.xn3,
                            in_offset=bass.IndirectOffsetOnAxis(ap=staged[:, k, q:q + 1], axis=0),
                        ).then_inc(gathered[k][q], 16)
            in_steps(pool, PG, 2, body, lead=2)

        @block.tensor
        def _(pe):
            t = nc.tensor

            def body(item, b):
                for q in range(GT):
                    it = item(1)
                    if it:
                        k = it.buf(2)
                        n = it.i * GT + q
                        pe.wait_ge(gathered[k][q], (it.turn(2) + 1) * 16)
                        at_least(pe, m.lo_ready, n)
                        for c in range(KD):
                            tr = t.transpose(turned[:, c // 4, (c % 4) * P:(c % 4 + 1) * P],
                                             rows[:, k, q, c * P:(c + 1) * P], g.ident[:])
                        tr.then_inc(m.turned_ready, 1)
                    it = item(2)
                    if it:
                        k = it.buf(2)
                        pe.wait_ge(m.split_ready, it.i + 1)
                        pe.wait_ge(m.raw2_used, it.i + 1)
                        at_least(pe, m.y_kept, it.i * GT + q - 1)
                        expert_output(t, y[:, q], h_hi, h_lo, w2_hi[:, k], w2_lo[:, k], q).then_inc(m.y_ready, 1)
                it = item(1)
                if it:
                    k = it.buf(2)
                    pe.wait_ge(m.lo_ready, (it.i + 1) * GT)
                    pe.wait_ge(m.raw1_used, it.i + 1)
                    at_least(pe, m.act_ready, it.i)
                    expert_hidden(t, hidden, w1_hi[:, k], w1_lo[:, k], hi, lo).then_inc(m.hidden_ready, 1)
            in_steps(pe, PG, 2, body, lead=2)

        @block.scalar
        def _(act):
            s = nc.scalar
            act.wait_ge(m.small_in, 32)

            def body(item, b):
                it = item(0)
                if it:
                    k = it.buf(2)
                    for q in range(GT):
                        at_least(act, gathered[k][q], it.turn(2) * 16)
                    act.sem_inc(m.pace, 1)
                    s.copy(staged[:, k, :], g.sorted_token[:, bass.ds(it.i * GT, GT)]).then_inc(m.staged_ready, 1)
                for q in range(GT):
                    it = item(1)
                    if it:
                        act.wait_ge(m.turned_ready, it.i * GT + q + 1)
                        at_least(act, m.hidden_ready, it.i)
                        s.copy(hi[:, :, q * P:(q + 1) * P],
                               turned[:].rearrange("p h (c n) -> p (h c) n", n=P)).then_inc(m.hi_ready, 1)
                it = item(0)
                if it:
                    k = it.buf(2)
                    act.wait_ge(m.raw1_in, (it.i + 1) * 16)
                    at_least(act, m.hidden_ready, it.i - 1)
                    s.copy(w1_hi[:, k].rearrange("p c f -> p (c f)"), raw1[:]).then_inc(m.w1_high, 1)
                    act.wait_ge(m.raw2_in, (it.i + 1) * 16)
                    at_least(act, m.y_ready, (it.i - 1) * GT)
                    s.copy(w2_hi[:, k].rearrange("p m n -> p (m n)"), raw2[:]).then_inc(m.w2_high, 1)
                it = item(1)
                if it:
                    k = it.buf(2)
                    e = act.value_load(g.expert[0:1, bass.ds(it.i, 1)], min_val=0, max_val=EXPERTS - 1)
                    act.sem_inc(m.pace, 1)
                    s.copy(bias1[:, k, :], all_bias1[:, bass.ds(e * 2, 2)]).then_inc(m.bias1_ready, 1)
                    act.wait_ge(m.hidden_ready, it.i + 1)
                    at_least(act, m.split_ready, it.i)
                    act.wait_ge(m.bias1_ready, it.i + 1)
                    for c in range(2):
                        cols = slice(c * GT * P, (c + 1) * GT * P)
                        ins = s.activation(act_out[:, cols], hidden[:, cols], ACT.Gelu, bias=bias1[:, k, c:c + 1])
                    ins.then_inc(m.act_ready, 1)
            in_steps(act, PG, 2, body, lead=2)

        @block.vector
        def _(dve):
            v = nc.vector
            st = Steps(dve, m.v_done)

            def body(item, b):
                for q in range(GT):
                    it = item(1)
                    if it:
                        dve.wait_ge(m.hi_ready, it.i * GT + q + 1)
                        tokens = slice(q * P, (q + 1) * P)
                        v.tensor_tensor(lo[:, :, tokens], turned[:].rearrange("p h (c n) -> p (h c) n", n=P),
                                        hi[:, :, tokens].bitcast(F32), ALU.subtract).then_inc(m.lo_ready, 1)
                    it = item(2)
                    if it:
                        k = it.buf(2)
                        dve.wait_ge(m.y_ready, it.i * GT + q + 1)
                        if q == 0:
                            dve.wait_ge(bias2_in[k], (it.turn(2) + 1) * 16)
                            at_least(dve, y_stored[k], it.turn(2) * 16)
                        v.tensor_tensor(y_out[:, k, q, :], y[:, q].rearrange("p h n -> p (h n)"), bias2[:, k, :],
                                        ALU.add).then_inc(m.y_kept, 1)
                it = item(0)
                if it:
                    k = it.buf(2)
                    dve.wait_ge(m.raw1_in, (it.i + 1) * 16)
                    dve.wait_ge(m.w1_high, it.i + 1)
                    split_vector(v, w1_lo[:, k].rearrange("p c f -> p (c f)"), raw1[:],
                                 w1_hi[:, k].rearrange("p c f -> p (c f)"), m.raw1_used)
                    dve.wait_ge(m.raw2_in, (it.i + 1) * 16)
                    dve.wait_ge(m.w2_high, it.i + 1)
                    split_vector(v, w2_lo[:, k].rearrange("p m n -> p (m n)"), raw2[:],
                                 w2_hi[:, k].rearrange("p m n -> p (m n)"), m.raw2_used)
                it = item(1)
                if it:
                    dve.wait_ge(m.act_ready, it.i + 1)
                    at_least(dve, m.y_ready, it.i * GT)
                    whole = act_out[:].rearrange("p (m n) -> p m n", m=2)
                    st.link(v.tensor_copy(h_hi[:], whole))
                    split_vector(v, h_lo[:], whole, h_hi[:], m.split_ready)
            in_steps(dve, PG, 2, body, st, 1, lead=2)



def stage_combine(nc, g):
    with ExitStack() as ctx:
        a = Alloc(nc, ctx)
        x4, ys = a.sb("c_x4", [P, 4, D]), a.sb("c_ys", [P, 4, TOPK, D])
        staged = a.sb("c_staged", [P, 4, TOPK], I32)
        x_in, out_done = [a.sem(f"c_x_in{k}") for k in range(4)], [a.sem(f"c_out_done{k}") for k in range(4)]
        gathered = [[a.sem(f"c_gathered{k}{q}") for q in range(TOPK)] for k in range(4)]
        staged_ready, added, v_done, pace = (a.sem(f"c_{n}") for n in ("staged_ready", "added", "v_done", "pace"))
        places = g.pair_place[:].rearrange("p (k t) -> p k t", k=TOPK)

        block = ctx.enter_context(nc.Block())

        @block.sync
        def _(sp):
            def body(item, b):
                it = item(0)
                if it:
                    k = it.buf(4)
                    at_least(sp, out_done[k], it.turn(4) * 16)
                    sp.dma_start(x4[:, k, :], g.x4[bass.ds(it.i * P, P), :]).then_inc(x_in[k], 16)
                it = item(3)
                if it:
                    k = it.buf(4)
                    n = LAST if isinstance(it.i, int) and it.i == NT - 1 else P
                    sp.wait_ge(added, it.i + 1)
                    sp.dma_start(g.out[bass.ds(it.i * P, n), :], x4[0:n, k, :]).then_inc(out_done[k], 16)
            in_steps(sp, NT, 4, body)
            for k in range(4):
                sp.wait_ge(out_done[k], 16 * (NT // 4))

        @block.scalar
        def _(act):
            def body(item, b):
                it = item(0)
                if it:
                    k = it.buf(4)
                    for q in range(TOPK):
                        at_least(act, gathered[k][q], it.turn(4) * 16)
                    act.sem_inc(pace, 1)
                    nc.scalar.copy(staged[:, k, :], places[:, :, bass.ds(it.i, 1)].rearrange("p k t -> p (k t)")).then_inc(staged_ready, 1)
            in_steps(act, NT, 4, body)

        @block.gpsimd
        def _(pool):
            def body(item, b):
                it = item(0)
                if it:
                    k = it.buf(4)
                    at_least(pool, added, it.i - 3)
                    pool.wait_ge(staged_ready, it.i + 1)
                    pool.sem_inc(pace, 1)
                    for q in range(TOPK):
                        pool.indirect_dma_start(
                            out=ys[:, k, q, :], out_offset=None, in_=g.y,
                            in_offset=bass.IndirectOffsetOnAxis(ap=staged[:, k, q:q + 1], axis=0),
                        ).then_inc(gathered[k][q], 16)
            in_steps(pool, NT, 4, body)

        @block.vector
        def _(dve):
            v = nc.vector
            st = Steps(dve, v_done)

            def body(item, b):
                it = item(0)
                if it:
                    k = it.buf(4)
                    dve.wait_ge(x_in[k], (it.turn(4) + 1) * 16)
                    for q in range(TOPK):
                        dve.wait_ge(gathered[k][q], (it.turn(4) + 1) * 16)
                        ins = v.scalar_tensor_tensor(out=x4[:, k, :], in0=ys[:, k, q, :],
                                                     scalar=g.top_prob[:, q, bass.ds(it.i, 1)], in1=x4[:, k, :],
                                                     op0=ALU.mult, op1=ALU.add)
                        if q == 0:
                            st.link(ins)
                    ins.then_inc(added, 1)
            in_steps(dve, NT, 4, body, st, 1)


def build(nc, x, src, dst, edge_weight, W0, ln1_g, ln1_b, w1, b1, ln2_g, ln2_b, w2, b2, W1, a_l, a_r,
          router_w, router_b, sw1, sb1, sw2, sb2, rw1, rb1, rw2, rb2, out):
    def scratch(name, shape):
        return nc.dram_tensor(name, shape, F32, kind="Internal").ap()

    g = Named(
        x=x, src_in=src, W0=W0, w1=w1, w2=w2, W1=W1, a_l=a_l, a_r=a_r, dst=dst, edge_weight=edge_weight,
        ln1_g=ln1_g, ln1_b=ln1_b, b1=b1, ln2_g=ln2_g, ln2_b=ln2_b, b2=b2, router_w=router_w, router_b=router_b,
        sw1=sw1, sb1=sb1, sw2=sw2, sb2=sb2, rw1=rw1, rb1=rb1, rw2=rw2, rb2=rb2, out=out,
        lists=[scratch(f"edge_list{k}", [P * NE, 4]) for k in range(LISTS)],
        z0=scratch("z0_rows", [NPAD, D]), z1=scratch("z1_rows", [NPAD, D]), el=scratch("el_rows", [NPAD, 4]),
        x2=scratch("x2_rows", [NPAD, D]), x4=scratch("x4_rows", [NPAD, D]), xn3=scratch("xn3_rows", [NPAD, D]), y=scratch("y_rows", [PT * P, D]),
    )
    with ExitStack() as ctx:
        a = Alloc(nc, ctx)
        g.eps = a.sb("eps", [P, 1])
        g.ident = a.sb("ident", [P, P])
        g.iota1 = a.sb("iota1", [P, P])
        g.src = a.sb("edge_src", [P, NE], I32)
        g.place = a.sb("edge_place", [P, NE])
        g.weight = a.sb("edge_weight_sorted", [P, NE])
        g.ntile = a.sb("group_ntile", [P, NG], I32)
        g.att_hi, g.att_lo = a.sb("att_hi", [P, KD, 8], F32R), a.sb("att_lo", [P, KD, 8], F32R)
        g.unit, g.scale = a.sb("unit", [P, 2]), a.sb("scale", [P, 2])
        shared = a.sb("shared", [P, D * HID // P])
        half = D * HID // P // 2
        g.t1 = shared[:, 0:half].bitcast(BF16).rearrange("p (c n) -> p c n", c=KD)
        g.t2 = shared[:, half:2 * half].bitcast(BF16).rearrange("p (c n) -> p c n", c=KH)
        ends = [NT * 2 * HEADS, NT * 3 * HEADS, NT * 3 * HEADS + NE * HEADS]
        g.scores = shared[:, 0:ends[0]].rearrange("p (t h) -> p t h", t=NT)
        g.sums = shared[:, ends[0]:ends[1]].rearrange("p (t h) -> p t h", t=NT)
        g.edge_el = shared[:, ends[1]:ends[2]].rearrange("p (t h) -> p t h", t=NE)
        stage_sort_and_project(nc, g)
        g.logits = a.sb("logits", [P, NT, EXPERTS])
        g.top_prob = a.sb("top_prob", [P, TOPK, NT])
        g.pair_place = a.sb("pair_place", [P, NPAIR], I32)
        g.expert = a.sb("group_expert", [P, PG], I32)
        g.sorted_token = a.sb("sorted_token", [P, PT], I32)
        with nc.sbuf_tensor("x_all", [P, NT, D], F32) as x_all:
            g.x_all = x_all
            stage_first_graph(nc, g)
            stage_first_ffn(nc, g)
            stage_attention_projection(nc, g)
            stage_attention_max(nc, g)
            stage_second_graph(nc, g)
            stage_shared_expert(nc, g)
        stage_route(nc, g)
        stage_experts(nc, g)
        stage_combine(nc, g)

_INS = ['x', 'src', 'dst', 'edge_weight', 'L0_gnn_W', 'L0_ffn_ln1_g', 'L0_ffn_ln1_b', 'L0_ffn_w1', 'L0_ffn_b1', 'L0_ffn_ln2_g', 'L0_ffn_ln2_b', 'L0_ffn_w2', 'L0_ffn_b2', 'L1_gnn_W', 'L1_gnn_a_l', 'L1_gnn_a_r', 'L1_ffn_router_w', 'L1_ffn_router_b', 'L1_ffn_sw1', 'L1_ffn_sb1', 'L1_ffn_sw2', 'L1_ffn_sb2', 'L1_ffn_rw1', 'L1_ffn_rb1', 'L1_ffn_rw2', 'L1_ffn_rb2']
_OUTS = [((2500, 1024), 'float32')]


def kernel(**inputs):
    import numpy as _np
    import concourse.bacc as _bacc
    from concourse import mybir as _mybir
    from concourse.bass_utils import run_bass_kernel_spmd as _run

    nc = _bacc.Bacc("TRN2", target_bir_lowering=False, num_devices=1)
    arrays, args = {}, []
    for name in _INS:
        a = _np.ascontiguousarray(inputs[name])
        arrays[f"in_{name}_dram"] = a
        args.append(nc.dram_tensor(f"in_{name}_dram", a.shape, _mybir.dt.from_np(a.dtype), kind="ExternalInput").ap())
    for i, (shape, dtype) in enumerate(_OUTS):
        dt = _mybir.dt.from_np(_np.dtype(dtype))
        args.append(nc.dram_tensor(f"out_{i}_dram", shape, dt, kind="ExternalOutput").ap())
    build(nc, *args)
    r = _run(nc, [arrays], core_ids=[0])
    got = tuple(r.results[0][f"out_{i}_dram"] for i in range(len(_OUTS)))
    return got[0]
```
